# Optimizing a Trainium2 kernel written in Bass

```python
import numpy as np
import jax
import jax.numpy as jnp

def _softmax(x, axis=-1):
    return jax.nn.softmax(x, axis=axis)

def _gelu(x):
    return jax.nn.gelu(x, approximate=True)

def _silu(x):
    return jax.nn.silu(x)

def _sigmoid(x):
    return jax.nn.sigmoid(x)

def _layernorm(x, axis=-1, eps=1e-05):
    m = jnp.mean(x, axis=axis, keepdims=True)
    v = jnp.var(x, axis=axis, keepdims=True)
    return (x - m) / jnp.sqrt(v + eps)

def _scatter_add(tgt, idx, src, axis=0):
    return tgt.at[idx].add(src)

def _segment_sum(src, seg, n):
    return jax.ops.segment_sum(src, seg, n)
kernel_name = 'mk_gps_d1_gnn_r8_156fc7'

def setup_inputs(seed: int=0):
    np.random.seed(seed)
    _w = jnp.asarray

    def _rec_inputs():
        import jax
        import jax.numpy as jnp
        _gk = jax.random.key(seed)
        x = -0.0002117 + 1 * jax.random.normal(jax.random.fold_in(_gk, 1), (6250, 256), jnp.float32)
        src = jax.random.randint(jax.random.fold_in(_gk, 2), (200000,), 0, 6250, jnp.int32)
        dst = jnp.minimum((6250 * jax.random.uniform(jax.random.fold_in(_gk, 3), (200000,)) ** 2.0).astype(jnp.int32), 49999)
        _o = jnp.argsort(dst, stable=True)
        src = src[_o]
        dst = dst[_o]
        return (x, src, dst)
    x, src, dst = _rec_inputs()

    def _L0_gnn_setup():
        import jax, jax.numpy as jnp
        import numpy as np
        N = 12500
        E = 200000
        IN_FEATS = 256
        OUT_FEATS = 256
        MAXK = 32

        def _maxk(x, k):
            _, idx = jax.lax.top_k(x, k)
            rows = jnp.arange(x.shape[0])[:, None]
            mask = jnp.zeros_like(x).at[rows, idx].set(1.0)
            return x * mask
        key = jax.random.key(seed)
        k1, k2, k3, k4, k5 = jax.random.split(key, 5)
        feat = jax.random.normal(k1, (N, IN_FEATS), dtype=jnp.float32)
        W_self = jax.random.normal(k2, (IN_FEATS, OUT_FEATS), dtype=jnp.float32) * (1.0 / np.sqrt(IN_FEATS))
        W_neigh = jax.random.normal(k3, (IN_FEATS, OUT_FEATS), dtype=jnp.float32) * (1.0 / np.sqrt(IN_FEATS))
        src = jax.random.randint(k4, (E,), 0, N, dtype=jnp.int64)
        dst = jax.random.randint(k5, (E,), 0, N, dtype=jnp.int64)
        return {'feat': feat, 'W_self': W_self, 'W_neigh': W_neigh, 'src': src, 'dst': dst}
    _L0_gnn_all = _L0_gnn_setup()
    _L0_gnn_in = {k: v for k, v in _L0_gnn_all.items() if k in ('W_self', 'W_neigh')}
    del _L0_gnn_all

    def _L0_mix_setup():
        import jax, jax.numpy as jnp
        import numpy as np
        B, N, C, H = (8, 2048, 256, 8)
        D = C // H
        GH = C // 4
        key = jax.random.key(seed)
        ks = jax.random.split(key, 6)
        s = 0.02
        return {'x': jax.random.normal(ks[0], (B, N, C), dtype=jnp.float32), 'Wqkv': jax.random.normal(ks[1], (C, 3 * C), dtype=jnp.float32) * s, 'Wproj': jax.random.normal(ks[2], (C, C), dtype=jnp.float32) * s, 'bproj': jnp.zeros((C,), dtype=jnp.float32), 'ln_g': jnp.ones((C,), dtype=jnp.float32), 'ln_b': jnp.zeros((C,), dtype=jnp.float32), 'Wg1': jax.random.normal(ks[3], (C, GH), dtype=jnp.float32) * s, 'bg1': jnp.zeros((GH,), dtype=jnp.float32), 'Wg2': jax.random.normal(ks[4], (GH, C), dtype=jnp.float32) * s, 'bg2': jnp.zeros((C,), dtype=jnp.float32)}
    _L0_mix_all = _L0_mix_setup()
    _L0_mix_in = {k: v for k, v in _L0_mix_all.items() if k in ('Wqkv', 'Wproj', 'bproj', 'ln_g', 'ln_b', 'Wg1', 'bg1', 'Wg2', 'bg2')}
    del _L0_mix_all

    def _L0_ffn_setup():
        import jax, jax.numpy as jnp
        import numpy as np
        B, S, D = (8, 512, 256)
        H = 4 * D
        CAPACITY = 0.5
        key = jax.random.key(seed)
        ks = jax.random.split(key, 6)
        x = jax.random.normal(ks[0], (B, S, D), dtype=jnp.float32)
        attention_mask = jnp.zeros((B, 1, 1, S), dtype=jnp.float32)
        wr = jax.random.normal(ks[1], (D, 1), dtype=jnp.float32) * 0.02
        br = jnp.zeros((1,), dtype=jnp.float32)
        w1 = jax.random.normal(ks[2], (D, H), dtype=jnp.float32) * 0.02
        b1 = jnp.zeros((H,), dtype=jnp.float32)
        w2 = jax.random.normal(ks[3], (H, D), dtype=jnp.float32) * 0.02
        b2 = jnp.zeros((D,), dtype=jnp.float32)
        return {'x': x, 'attention_mask': attention_mask, 'wr': wr, 'br': br, 'w1': w1, 'b1': b1, 'w2': w2, 'b2': b2}
    _L0_ffn_all = _L0_ffn_setup()
    _L0_ffn_in = {k: v for k, v in _L0_ffn_all.items() if k in ('attention_mask', 'wr', 'br', 'w1', 'b1', 'w2', 'b2')}
    del _L0_ffn_all
    return {'x': x, 'src': src, 'dst': dst, 'L0_gnn_W_self': _L0_gnn_in['W_self'], 'L0_gnn_W_neigh': _L0_gnn_in['W_neigh'], 'L0_mix_Wqkv': _L0_mix_in['Wqkv'], 'L0_mix_Wproj': _L0_mix_in['Wproj'], 'L0_mix_bproj': _L0_mix_in['bproj'], 'L0_mix_ln_g': _L0_mix_in['ln_g'], 'L0_mix_ln_b': _L0_mix_in['ln_b'], 'L0_mix_Wg1': _L0_mix_in['Wg1'], 'L0_mix_bg1': _L0_mix_in['bg1'], 'L0_mix_Wg2': _L0_mix_in['Wg2'], 'L0_mix_bg2': _L0_mix_in['bg2'], 'L0_ffn_attention_mask': _L0_ffn_in['attention_mask'], 'L0_ffn_wr': _L0_ffn_in['wr'], 'L0_ffn_br': _L0_ffn_in['br'], 'L0_ffn_w1': _L0_ffn_in['w1'], 'L0_ffn_b1': _L0_ffn_in['b1'], 'L0_ffn_w2': _L0_ffn_in['w2'], 'L0_ffn_b2': _L0_ffn_in['b2']}

def reference(x, src, dst, L0_gnn_W_self, L0_gnn_W_neigh, L0_mix_Wqkv, L0_mix_Wproj, L0_mix_bproj, L0_mix_ln_g, L0_mix_ln_b, L0_mix_Wg1, L0_mix_bg1, L0_mix_Wg2, L0_mix_bg2, L0_ffn_attention_mask, L0_ffn_wr, L0_ffn_br, L0_ffn_w1, L0_ffn_b1, L0_ffn_w2, L0_ffn_b2):
    import jax
    import jax.numpy as jnp

    def _L0_gnn_ref(feat, W_self, W_neigh, src, dst):
        import jax, jax.numpy as jnp
        import numpy as np
        N = 12500
        E = 200000
        IN_FEATS = 256
        OUT_FEATS = 256
        MAXK = 32

        def _maxk(x, k):
            _, idx = jax.lax.top_k(x, k)
            rows = jnp.arange(x.shape[0])[:, None]
            mask = jnp.zeros_like(x).at[rows, idx].set(1.0)
            return x * mask
        n = feat.shape[0]
        h_self = feat @ W_self
        h_neigh = feat @ W_neigh
        h_sparse = _maxk(h_neigh, MAXK)
        msg = h_sparse[src]
        summed = jax.ops.segment_sum(msg, dst, num_segments=n)
        deg = jax.ops.segment_sum(jnp.ones((src.shape[0],), dtype=feat.dtype), dst, num_segments=n)
        neigh = summed / jnp.maximum(deg, 1.0)[:, None]
        return h_self + neigh

    def _L0_mix_ref(x, Wqkv, Wproj, bproj, ln_g, ln_b, Wg1, bg1, Wg2, bg2):
        import jax, jax.numpy as jnp
        import numpy as np
        B, N, C, H = (8, 2048, 256, 8)
        D = C // H
        GH = C // 4
        b, n, c = x.shape
        h, d = (H, D)
        qkv = (x @ Wqkv).reshape(b, n, 3, h, d)
        q, k, v = (qkv[:, :, 0], qkv[:, :, 1], qkv[:, :, 2])
        k = jax.nn.softmax(k, axis=1)
        context = jnp.einsum('bnhd,bnhv->bhdv', k, v)
        out = jnp.einsum('bnhd,bhdv->bnhv', q, context).reshape(b, n, c)
        mu = jnp.mean(x, axis=-1, keepdims=True)
        var = jnp.var(x, axis=-1, keepdims=True)
        xn = (x - mu) * jax.lax.rsqrt(var + 1e-05) * ln_g + ln_b
        hgate = jax.nn.gelu(xn @ Wg1 + bg1, approximate=False)
        gate = jax.nn.sigmoid(hgate @ Wg2 + bg2)
        return out * gate @ Wproj + bproj

    def _L0_ffn_ref(x, attention_mask, wr, br, w1, b1, w2, b2):
        import jax, jax.numpy as jnp
        import numpy as np
        B, S, D = (8, 512, 256)
        H = 4 * D
        CAPACITY = 0.5
        b, s, d = x.shape
        weights = (jnp.einsum('bsd,do->bso', x, wr) + br)[..., 0]
        k = max(1, int(CAPACITY * s))
        kk = k - 1 if k > 1 else 1
        _, idx = jax.lax.top_k(weights, k)
        sel_idx = idx[:, :kk]
        sel = jnp.take_along_axis(x, sel_idx[:, :, None], axis=1)
        h = jax.nn.gelu(jnp.einsum('bkd,dh->bkh', sel, w1) + b1)
        y = jnp.einsum('bkh,hd->bkd', h, w2) + b2
        w_sel = jnp.take_along_axis(weights, sel_idx, axis=1)
        y = y * w_sel[..., None]
        batch_idx = jnp.arange(b)[:, None]
        processed = jnp.zeros_like(x).at[batch_idx, sel_idx].set(y)
        return processed + x
    xn = _layernorm(x, axis=-1)
    x = x + _L0_gnn_ref(xn, L0_gnn_W_self, L0_gnn_W_neigh, src, dst) + _L0_mix_ref(xn[None], L0_mix_Wqkv, L0_mix_Wproj, L0_mix_bproj, L0_mix_ln_g, L0_mix_ln_b, L0_mix_Wg1, L0_mix_bg1, L0_mix_Wg2, L0_mix_bg2)[0]
    x = x + _L0_ffn_ref(_layernorm(x, axis=-1)[None], L0_ffn_attention_mask, L0_ffn_wr, L0_ffn_br, L0_ffn_w1, L0_ffn_b1, L0_ffn_w2, L0_ffn_b2)[0]
    return x

_drawn_inputs = setup_inputs


def setup_inputs(seed=0):
    import zlib

    import numpy as np

    out = dict(_drawn_inputs(seed))
    spreads = {'L0_mix_bproj': (0.0, 0.8),
     'L0_mix_ln_g': (1.0, 0.6),
     'L0_mix_ln_b': (0.0, 0.8),
     'L0_mix_bg1': (0.0, 0.8),
     'L0_mix_bg2': (0.0, 0.8),
     'L0_ffn_b1': (0.0, 0.8),
     'L0_ffn_b2': (0.0, 0.77)}
    factors = {'L0_mix_Wqkv': 8.0,
     'L0_mix_Wproj': 8.0,
     'L0_mix_Wg1': 8.0,
     'L0_mix_Wg2': 8.0,
     'L0_ffn_wr': 4.632,
     'L0_ffn_w1': 4.853,
     'L0_ffn_w2': 4.535,
     'L0_gnn_W_neigh': 6.179}
    for name, (base, spread) in spreads.items():
        noise = np.random.default_rng([zlib.crc32(name.encode()), seed]).standard_normal(out[name].shape)
        drawn = base * np.exp(spread * noise) if base else spread * noise
        out[name] = jnp.asarray(drawn.astype(out[name].dtype))
    for name, factor in factors.items():
        out[name] = (out[name] * factor).astype(out[name].dtype)
    return out
```

```python
from contextlib import ExitStack

import concourse.bass as bass
from concourse import mybir

F32 = mybir.dt.float32
F16 = mybir.dt.float16
I32 = mybir.dt.int32
ALU = mybir.AluOpType
ACT = mybir.ActivationFunctionType
AX_X = mybir.AxisListType.X

EPS = 1e-5
TOPK = 32
BELOW = -3.0e38
NOWHERE = 1 << 20
LO_SCALE = 4096.0


class Steps:

    def __init__(self, engine, semaphore, base=0, alone=None):
        self.engine, self.semaphore, self.base, self.alone, self.n = engine, semaphore, base, alone, 0

    def mark(self, instruction):
        instruction.then_inc(self.semaphore, 1)
        self.n += 1
        return self.n

    def after(self, n):
        self.engine.wait_ge(self.semaphore, self.base + n)
        if self.alone is not None:
            self.engine.sem_inc(self.alone, 1)


def build(nc, x_d, src_d, dst_d, w_self_d, w_neigh_d, wqkv_d, wproj_d, bproj_d, ln_g_d, ln_b_d, wg1_d, bg1_d,
          wg2_d, bg2_d, mask_d, wr_d, br_d, w1_d, b1_d, w2_d, b2_d, out_d):
    N, C = x_d.shape
    E = src_d.shape[0]
    T = 125
    NT = N // T
    KC = C // 128
    GH = wg1_d.shape[1]
    HID = w1_d.shape[1]
    NH = HID // 128
    HD = 32
    KEEP = N // 2 - 1
    BODY = 10
    assert NT * T == N and NT % BODY == 0 and C == 256

    CHUNK = 128
    GC = 4
    RING = 8
    ROUNDS = -(-E // (CHUNK * GC * RING))
    NG = ROUNDS * RING
    CH = NG * GC
    assert (NG - 1) * GC * CHUNK >= E
    FULL = E // CHUNK
    REST = E - FULL * CHUNK
    BL = -(-(FULL + 1) // 128)
    TAIL = FULL - (BL - 1) * 128
    XL = NT // 5

    with ExitStack() as ctx:
        def sb(name, shape, dt=F32):
            return ctx.enter_context(nc.sbuf_tensor(name, shape, dt))

        def sem(name):
            return ctx.enter_context(nc.semaphore(name))

        s_alone = sem("s_alone")

        def hold(engine, semaphore, value):
            engine.wait_ge(semaphore, value)
            engine.sem_inc(s_alone, 1)

        class Region:

            def __init__(self, name, words):
                self.mem, self.at, self.words = sb(name, [128, words]), 0, words

            def take(self, shape, dt=F32):
                n = 1
                for s in shape[1:]:
                    n *= s
                words = n // 2 if dt == F16 else n
                assert self.at + words <= self.words
                ap = self.mem[0:shape[0], self.at:self.at + words]
                self.at += words
                if dt != F32:
                    ap = ap.bitcast(dt)
                if len(shape) == 3:
                    ap = ap.rearrange("p (a b) -> p a b", a=shape[1])
                if len(shape) == 4:
                    ap = ap.rearrange("p (a b c) -> p a b c", a=shape[1], b=shape[2])
                return ap

        region_k = Region("region_k", (NT + 1) * C)
        dst_raw = region_k.take([128, BL, 128], I32)
        nxt_raw = region_k.take([128, BL, 128], I32)
        src_raw = region_k.take([128, BL, 128], I32)
        dst_f = region_k.take([128, BL, 128])
        src_f = region_k.take([128, BL, 128])
        falls = region_k.take([128, BL, 128])
        k_all = region_k.mem[0:T, 0:NT * C].rearrange("p (t c) -> p t c", c=C)
        yw_all = region_k.mem[0:T, :].rearrange("p (t c) -> p t c", c=C)

        VH = 130
        VW = KC * VH
        region_v = Region("region_v", (NT + 2) * VW)
        x_all = region_v.mem[0:T, :].rearrange("p (t w) -> p t w", w=VW)
        v_all = region_v.mem[0:T, :].rearrange("p (t h w) -> p t h w", h=KC, w=VH)
        w1 = region_v.take([128, KC, HID])
        w2 = region_v.take([128, NH, C])
        w_self = region_v.take([128, KC, C])
        wproj = region_v.take([128, KC, C])
        w_out = region_v.take([128, KC, C])
        b2 = region_v.take([T, C])
        bproj = region_v.take([T, C])
        wr = region_v.take([T, C])
        xin = region_v.take([T, C])
        agg_sum = region_v.take([T, C])
        base_x = region_v.take([T, C])
        base_p = region_v.take([T, C])
        x2 = region_v.take([T, C])
        x3 = region_v.take([T, C])
        gate = region_v.take([T, C])
        mixed = region_v.take([T, C])
        ybias = region_v.take([T, C])
        junk = region_v.take([T, C])
        mixT = region_v.take([128, KC, T])
        x3T = region_v.take([128, KC, T])
        xTc = region_v.take([128, KC, T])
        hidT = region_v.take([128, NH, T])
        hgT = region_v.take([GH + 1, T])
        hg_pre = region_v.take([T, GH])
        hg = region_v.take([T, GH])
        wv = region_v.take([T, NT])
        hit = region_v.take([T, NT])
        hit_n = region_v.take([T, 7, NT])
        eqm = region_v.take([T, NT])
        gtm = region_v.take([T, NT])
        selm = region_v.take([T, NT])
        colcum = region_v.take([T, NT])
        ones_row = region_v.take([T, NT])
        prefix = region_v.take([T, NT])
        cand = region_v.take([T, 8], I32)
        digits = region_v.take([T, 8], I32)
        counts = region_v.take([T, 8])
        over = region_v.take([T, 8])

        region_r = Region("region_r", NT * C)
        res_all = region_r.mem[0:T, :].rearrange("p (t c) -> p t c", c=C)
        w_neigh = region_r.take([128, KC, C])
        wkv = region_r.take([128, KC, 2 * C])
        wq = region_r.take([128, KC, C])
        wqT = region_r.take([128, KC, C])
        kdiag = region_r.take([128, KC, 128])
        ek = region_r.take([T, 2, 5 * C])
        xn = region_r.take([T, 2, C])
        xT = region_r.take([128, 2, KC * T])
        taken = region_r.take([T, 2, C])
        sparse = region_r.take([T, 2, C])
        rest32 = region_r.take([T, C])
        split16 = region_r.take([T, 2, 2 * C], F16)
        top8 = region_r.take([T, 2 * (TOPK // 8), 8])
        kparts = region_r.take([T, NT // BODY, C])
        kmax = region_r.take([T, C])
        kmaxb = region_r.take([T, C])
        stats = region_r.take([T, NT, 6])
        mean = region_r.take([T, NT])
        var = region_r.take([T, NT])
        sums = region_r.take([T, NT])
        diff = region_r.take([T, NT])
        var2 = region_r.take([T, NT])
        std1 = region_r.take([T, NT])
        std1b = region_r.take([T, NT])
        stdg = region_r.take([T, NT])
        below = region_r.take([NT + 1, NG])
        last_row = region_r.take([128, NT + 1])
        ln_bT = region_r.take([128, KC, T])
        wg1 = region_r.take([128, KC, GH])

        ring = sb("ring", [128, RING * GC, 2 * C], F16)
        dstT = sb("dstT", [128, GC + CH])
        srcT = sb("srcT", [128, CH + GC], I32)
        stage = sb("stage", [128, RING * GC], I32)
        bounds = sb("bounds", [1, 3 * (NT + 1)], I32)
        ident = sb("ident", [128, 128])
        ones = sb("ones", [128, 128])
        upper = sb("upper", [T, T])
        iota = sb("iota", [128, T], F16)
        tile_base = sb("tile_base", [128, 1])
        zeros16 = sb("zeros16", [128, 2 * C], F16)
        ones16 = sb("ones16", [128, 2], F16)
        onehot = sb("onehot", [128, GC, T], F16)
        rstd = sb("rstd", [T, NT + 2])
        shift = sb("shift", [T, NT + 2])
        gate_scale = sb("gate_scale", [T, NT + 2])
        kmaxT = sb("kmaxT", [128, KC])
        ctx_bd = sb("ctx_bd", [128, KC, 128])
        ctx_r = sb("ctx_r", [128, KC])
        wg1g = sb("wg1g", [128, KC, GH])
        wg2 = sb("wg2", [GH + 1, C])
        bg1 = sb("bg1", [T, GH])
        bg1_row = sb("bg1_row", [1, GH])
        ln_g = sb("ln_g", [128, KC])
        ln_b = sb("ln_b", [128, KC])
        br = sb("br", [T, 1])
        b1 = sb("b1", [128, NH])
        eps = sb("eps", [T, 1])
        w_all = sb("w_all", [T, NT + 1])
        small = sb("small", [128, 16])
        tile_edge = sb("tile_edge", [NT + 1, 1])
        tile_flat = sb("tile_flat", [NT + 1, 1])
        bcol = sb("bcol", [NT + 1, 3])
        bn6 = sb("bn6", [T, 6])
        mv = sb("mv", [T, 2])
        col = {n: sb("col_" + n, [T, 1]) for n in (
            "std", "rstd", "deg", "rdeg", "w", "cnt", "pos", "sgn", "goal", "bit", "thr", "need")}
        best = sb("best", [T, 1], I32)
        accept = sb("accept", [T, 1], I32)

        bank = [ctx.enter_context(nc.psum_tensor(f"bank{i}", [128, 512], F32)) for i in range(8)]
        rows_d = nc.dram_tensor("rows_d", (N, 2 * C), F16).ap()
        xT_d = nc.dram_tensor("xT_d", (NT + 1, 128, KC * T), F32).ap()

        s_const, s_setup, s_edges, s_small = sem("s_const"), sem("s_setup"), sem("s_edges"), sem("s_small")
        s_xload = [sem(f"s_xload{i}") for i in range(5)]
        s_wA, s_wC, s_wF = sem("s_wA"), sem("s_wC"), sem("s_wF")
        s_pool = sem("s_pool")
        s_vec = [sem(f"s_vec{i}") for i in range(5)]
        s_edge_f, s_tr, s_dstc, s_srcc = sem("s_edge_f"), sem("s_tr"), sem("s_dstc"), sem("s_srcc")
        s_last, s_lastb, s_bcol, s_brow, s_bounds = sem("s_last"), sem("s_lastb"), sem("s_bcol"), sem("s_brow"), sem("s_bounds")
        s_var, s_std, s_norm = sem("s_var"), sem("s_std"), sem("s_norm")
        s_xn, s_xT, s_xTc, s_h, s_kv, s_kvc, s_km = (sem(n) for n in ("s_xn", "s_xT", "s_xTc", "s_h", "s_kv", "s_kvc", "s_km"))
        s_vones = sem("s_vones")
        s_sparse, s_split = sem("s_sparse"), sem("s_split")
        s_xTout = [sem("s_xTout0"), sem("s_xTout1")]
        s_rows = [sem("s_rows0"), sem("s_rows1")]
        s_kmT, s_dg, s_kmb, s_ksub, s_kexp, s_ekfree = (sem(n) for n in ("s_kmT", "s_dg", "s_kmb", "s_ksub", "s_kexp", "s_ekfree"))
        s_ctx, s_bd, s_wqT, s_wqTc, s_wout, s_woutc = (sem(n) for n in ("s_ctx", "s_bd", "s_wqT", "s_wqTc", "s_wout", "s_woutc"))
        s_wprep, s_bg1, s_ready = sem("s_wprep"), sem("s_bg1"), sem("s_ready")
        s_land = [sem(f"s_land{i}") for i in range(RING * GC)]
        s_landed, s_slot_free, s_stage = sem("s_landed"), sem("s_slot_free"), sem("s_stage")
        s_oh, s_oh_free, s_base, s_agg = sem("s_oh"), sem("s_oh_free"), sem("s_base"), sem("s_agg")
        s_xin, s_xTl, s_og, s_hgpre, s_hg, s_thg, s_hgT = (
            sem(n) for n in ("s_xin", "s_xTl", "s_og", "s_hgpre", "s_hg", "s_thg", "s_hgT"))
        s_g2, s_gate, s_mix, s_tm, s_mixT, s_p = (sem(n) for n in ("s_g2", "s_gate", "s_mix", "s_tm", "s_mixT", "s_p"))
        s_deg, s_v2, s_std2, s_x3, s_tx3, s_x3T = (sem(n) for n in ("s_deg", "s_v2", "s_std2", "s_x3", "s_tx3", "s_x3T"))
        s_f1a, s_f1b, s_hidT, s_y, s_yw = (sem(n) for n in ("s_f1a", "s_f1b", "s_hidT", "s_y", "s_yw"))
        s_cnt, s_tot, s_fin, s_res = sem("s_cnt"), sem("s_tot"), sem("s_fin"), sem("s_res")
        s_lastrow, s_stats, s_gs, s_kpart, s_bg1c = (sem(n) for n in ("s_lastrow", "s_stats", "s_gs", "s_kpart", "s_bg1c"))
        s_out = sem("s_out")

        x_t = x_d.rearrange("(t p) c -> p t c", p=T)
        out_t = out_d.rearrange("(t p) c -> p t c", p=T)
        rows_t = rows_d.rearrange("(t p) c -> p t c", p=T)
        xT_t = xT_d.rearrange("t p w -> p t w")
        SMALL = 8 * 16
        SETUP = 15
        DIGIT = 3
        ROUNDS_D = 10
        CANDS = 2 ** DIGIT - 1
        STEPS_A = (BODY // 2) * 2 * 2 * (TOPK // 8)
        STEPS_C = 13
        STEPS_D = 7
        PASSES = 2 * (NT + 1)

        def h_psum(s):
            return bank[3 + s // 2][0:T, (s % 2) * C:(s % 2 + 1) * C]

        def xT_psum(s):
            return bank[0][:, (s % 2) * C:(s % 2) * C + KC * T]

        block = ctx.enter_context(nc.Block())

        @block.sync
        def _(sp):
            for p in range(2):
                sp.sem_inc(s_rows[p], 16)
                sp.sem_inc(s_xTout[p], 16)
            sp.wait_ge(s_const, 4)
            full = (BL - 1) * 128 * 128
            for raw, d, o in ((dst_raw, dst_d, 0), (nxt_raw, dst_d, 1), (src_raw, src_d, 0)):
                sp.dma_start(raw[:, 0:BL - 1, :],
                             d[o:o + full].rearrange("(b r e) -> r b e", r=128, e=128)).then_inc(s_edges, 16)
                sp.dma_start(raw[0:TAIL, BL - 1, :],
                             d[full + o:full + o + TAIL * 128].rearrange("(r e) -> r e", e=128)).then_inc(s_edges, 16)
                sp.dma_start(raw[TAIL:TAIL + 1, BL - 1, 0:REST - o],
                             d[full + o + TAIL * 128:E].rearrange("(a e) -> a e", a=1)).then_inc(s_edges, 16)
            for i in range(5):
                sp.dma_start(x_all[:, i * XL:(i + 1) * XL, 0:C], x_t[:, i * XL:(i + 1) * XL, :]).then_inc(s_xload[i], 16)
            sp.dma_start(w_neigh, w_neigh_d.rearrange("(k p) n -> p k n", p=128)).then_inc(s_wA, 16)
            sp.dma_start(wkv, wqkv_d[:, C:3 * C].rearrange("(k p) n -> p k n", p=128)).then_inc(s_wA, 16)
            sp.dma_start(wq, wqkv_d[:, 0:C].rearrange("(k p) n -> p k n", p=128)).then_inc(s_wC, 16)
            with sp.Fori(0, NT // 2) as i:
                for p in range(2):
                    sp.wait_ge(s_split, i * 2 + p + 1 + 2)
                    sp.dma_start(rows_t[:, bass.ds(i * 2 + p, 1), :], split16[:, p:p + 1, :]).then_inc(s_rows[p], 16)
            sp.wait_ge(s_ctx, 1)
            for dst, src in ((w_self, w_self_d.rearrange("(k p) n -> p k n", p=128)),
                             (wproj, wproj_d.rearrange("(k p) n -> p k n", p=128)),
                             (bproj, bproj_d.partition_broadcast(T)),
                             (b2, b2_d.partition_broadcast(T)),
                             (wr, wr_d.rearrange("n a -> (n a)").partition_broadcast(T)),
                             (w1, w1_d.rearrange("(k p) n -> p k n", p=128)),
                             (w2, w2_d.rearrange("(k p) n -> p k n", p=128))):
                sp.dma_start(dst, src).then_inc(s_wF, 16)
            sp.wait_ge(s_bounds, 1)
            passes = sp.value_load(bounds[0:1, PASSES:PASSES + 1], min_val=1, max_val=NT)
            with sp.Fori(0, passes) as r:
                with sp.Fori(0, ROUNDS) as j:
                    for q in range(RING):
                        for s in range(GC):
                            sp.wait_ge(s_land[q * GC + s], (r * ROUNDS + j + 1) * 16)
                        sp.sem_inc(s_landed, 1)
            for i in range(5):
                sp.wait_ge(s_fin, XL * (i + 1))
                sp.dma_start(out_t[:, i * XL:(i + 1) * XL, :], res_all[:, i * XL:(i + 1) * XL, :]).then_inc(s_out, 16)
            sp.wait_ge(s_out, 16 * 5)

        @block.gpsimd
        def _(pool):
            pool.sem_inc(s_split, 2)
            pool.memset(dst_raw[:, BL - 1, :], NOWHERE).then_inc(s_const, 1)
            pool.memset(nxt_raw[:, BL - 1, :], NOWHERE).then_inc(s_const, 1)
            pool.memset(src_raw[:, BL - 1, :], 0).then_inc(s_const, 1)
            pool.memset(x_all[:, NT:NT + 2, :], 0.0).then_inc(s_const, 1)
            for dst, src in ((ln_g[:], ln_g_d.rearrange("(k p) -> p k", p=128)),
                             (ln_b[:], ln_b_d.rearrange("(k p) -> p k", p=128)),
                             (b1[:], b1_d.rearrange("(k p) -> p k", p=128)),
                             (wg1, wg1_d.rearrange("(k p) n -> p k n", p=128)),
                             (wg2[0:GH, :], wg2_d),
                             (wg2[GH:GH + 1, :], bg2_d.rearrange("(a n) -> a n", a=1)),
                             (bg1_row[:], bg1_d.rearrange("(a n) -> a n", a=1)),
                             (br[:], br_d.partition_broadcast(T))):
                with nc.allow_non_contiguous_dma(reason="a few hundred words, once"):
                    pool.dma_start(dst, src).then_inc(s_small, 16)
            pool.memset(ident[:], 0.0).then_inc(s_pool, 1)
            pool.memset(upper[:], 1.0).then_inc(s_pool, 1)
            pool.wait_ge(s_pool, 2)
            pool.affine_select(out=ident[:], in_=ident[:], compare_op=ALU.not_equal, fill=1.0, base=0,
                               pattern=[[-1, 128]], channel_multiplier=1).then_inc(s_setup, 1)
            pool.affine_select(out=upper[:], in_=upper[:], compare_op=ALU.is_gt, fill=0.0, base=0,
                               pattern=[[1, T]], channel_multiplier=-1).then_inc(s_setup, 1)
            pool.iota(iota[:], [[1, T]], base=0, channel_multiplier=0,
                      allow_small_or_imprecise_dtypes=True).then_inc(s_setup, 1)
            pool.iota(tile_edge[:], [[0, 1]], base=0, channel_multiplier=T,
                      allow_small_or_imprecise_dtypes=True).then_inc(s_setup, 1)
            pool.iota(tile_flat[:], [[0, 1]], base=0, channel_multiplier=NG,
                      allow_small_or_imprecise_dtypes=True).then_inc(s_setup, 1)
            for ap, value in ((ones[:], 1.0), (zeros16[:], 0.0), (ones16[:], 1.0), (eps[:], EPS), (w_all[:], 0.0),
                              (gate_scale[:], 1.0), (rstd[:], 1.0), (shift[:], 0.0), (ctx_bd[:], 0.0),
                              (dstT[:, 0:GC], float(NOWHERE))):
                pool.memset(ap, value).then_inc(s_setup, 1)
            pool.memset(srcT[:, CH:], 0).then_inc(s_pool, 1)
            with pool.Fori(0, NT // 2) as i:
                for p in range(2):
                    t = i * 2 + p
                    pool.wait_ge(s_sparse, t + 1 + BODY)
                    hold(pool, s_rows[p], (i + 1) * 16)
                    st = Steps(pool, s_pool, t * 2 + 3, s_alone)
                    a = st.mark(pool.tensor_copy(split16[:, p, 0:C], sparse[:, p, :]))
                    st.after(a)
                    a = st.mark(pool.tensor_tensor(rest32, sparse[:, p, :], split16[:, p, 0:C], ALU.subtract))
                    st.after(a)
                    pool.tensor_scalar(split16[:, p, C:2 * C], rest32, LO_SCALE, None, ALU.mult).then_inc(s_split, 1)
            for p in range(2):
                pool.wait_ge(s_rows[p], 16 * (NT // 2 + 1))
            pool.wait_ge(s_srcc, BL)
            pool.wait_ge(s_bounds, 1)
            passes = pool.value_load(bounds[0:1, PASSES:PASSES + 1], min_val=1, max_val=NT)
            pool.wait_ge(s_slot_free, 1)
            pool.tensor_copy(stage[:, 0:GC], srcT[:, 0:GC]).then_inc(s_stage, 1)
            with pool.Fori(0, passes) as r:
                with pool.Fori(0, ROUNDS) as j:
                    for q in range(RING):
                        g = (r * ROUNDS + j) * RING + q
                        hold(pool, s_slot_free, g + 2)
                        nx = (q + 1) % RING * GC
                        pool.tensor_copy(stage[:, nx:nx + GC],
                                         srcT[:, bass.ds((j * RING + q + 1) * GC, GC)]).then_inc(s_stage, 1)
                        hold(pool, s_stage, g + 1)
                        for s in range(GC):
                            c = q * GC + s
                            pool.indirect_dma_start(
                                out=ring[:, c, :], out_offset=None, in_=rows_d,
                                in_offset=bass.IndirectOffsetOnAxis(ap=stage[:, c:c + 1], axis=0)).then_inc(s_land[c], 16)

        @block.scalar
        def _(act):
            act.sem_inc(s_hidT, 2)
            for b in range(BL):
                w = min(128, CH - b * 128)
                act.wait_ge(s_tr, 2 * b + 2)
                act.activation(srcT[:, b * 128:b * 128 + w], bank[2 + b % 2][:, 0:w], ACT.Copy).then_inc(s_srcc, 1)
            act.wait_ge(s_setup, SETUP)
            act.wait_ge(s_var, 1)
            act.activation(std1, var, ACT.Sqrt, bias=eps[:, 0:1]).then_inc(s_std, 1)
            act.wait_ge(s_var, 2)
            act.activation(stdg, var2, ACT.Sqrt, bias=eps[:, 0:1]).then_inc(s_std, 1)
            act.wait_ge(s_norm, 1)

            def normalise(t, p):
                act.activation(xn[:, p, :].rearrange("p (a c) -> p a c", a=1), x_all[:, bass.ds(t, 1), 0:C], ACT.Identity,
                               bias=shift[:, bass.ds(t, 1)], scale=rstd[:, bass.ds(t, 1)]).then_inc(s_xn, 1)

            def keep_xT(t, p):
                act.wait_ge(s_xT, t + 1)
                act.activation(xT[:, p, :], xT_psum(p), ACT.Copy).then_inc(s_xTc, 1)

            def store_xT(t, p):
                act.wait_ge(s_xTc, t + 1)
                act.dma_start(xT_t[:, bass.ds(t, 1), :], xT[:, p:p + 1, :]).then_inc(s_xTout[p], 16)

            normalise(0, 0)
            keep_xT(0, 0)
            normalise(1, 1)
            store_xT(0, 0)
            act.sem_inc(s_kvc, 2)
            with act.Fori(0, NT // BODY) as i:
                for s in range(BODY):
                    t, p = i * BODY + s, (s + 1) % 2
                    act.wait_ge(s_xTout[p], (i * (BODY // 2) + (s + 1) // 2 + 1) * 16)
                    keep_xT(t + 1, p)
                    normalise(t + 2, s % 2)
                    store_xT(t + 1, p)
                    act.wait_ge(s_kv, t + 1)
                    kv = bank[1 + s % 2]
                    act.activation(k_all[:, bass.ds(t, 1), :], kv[0:T, 0:C].rearrange("p (a c) -> p a c", a=1), ACT.Copy)
                    act.activation(v_all[:, bass.ds(t, 1), :, 0:128],
                                   kv[0:T, C:2 * C].rearrange("p (a h c) -> p a h c", a=1, h=KC), ACT.Copy).then_inc(s_kvc, 1)
            with act.Fori(0, NT // 10) as i:
                for p in range(2):
                    act.wait_ge(s_ksub, i * 2 + p + 1)
                    act.wait_ge(s_ekfree, i * 2 + p + 1)
                    act.activation(ek[:, p, :], region_k.mem[0:T, bass.ds((i * 2 + p) * (5 * C), 5 * C)], ACT.Exp).then_inc(s_kexp, 1)
            act.wait_ge(s_wqT, 1)
            act.activation(wqT, bank[6][:, :].rearrange("p (k c) -> p k c", k=KC), ACT.Copy).then_inc(s_wqTc, 1)
            act.wait_ge(s_wout, 1)
            act.activation(w_out, bank[7][:, :].rearrange("p (k c) -> p k c", k=KC), ACT.Copy).then_inc(s_woutc, 1)
            act.wait_ge(s_ready, 1)

            def load_xT(j):
                act.dma_start(xTc.rearrange("p k t -> p (k t)"), xT_t[:, bass.ds(j, 1), :].rearrange("p a w -> p (a w)"))\
                   .then_inc(s_xTl, 16)

            def gate_hidden(j):
                act.wait_ge(s_hgpre, j + 1)
                act.activation(hg, hg_pre, ACT.Gelu).then_inc(s_hg, 1)
                act.wait_ge(s_thg, j + 1)
                act.activation(hgT[0:GH, :], bank[5][0:GH, C:C + T], ACT.Copy).then_inc(s_hgT, 1)

            def gate_open(j):
                act.wait_ge(s_g2, j + 1)
                act.activation(gate, bank[5][0:T, 0:C], ACT.Tanh, scale=0.5).then_inc(s_gate, 1)

            def mix_turned(j):
                act.wait_ge(s_tm, j + 1)
                act.activation(mixT, bank[3][:, 0:KC * T].rearrange("p (k t) -> p k t", k=KC), ACT.Copy).then_inc(s_mixT, 1)

            def hidden(i, half):
                act.wait_ge((s_f1a, s_f1b)[half], i + 1)
                for b in range(NH // 2):
                    n = half * (NH // 2) + b
                    last = act.activation(hidT[:, n, :], bank[(7, 4)[half]][:, b * T:(b + 1) * T],
                                          ACT.Gelu_apprx_tanh, bias=b1[:, n:n + 1])
                last.then_inc(s_hidT, 1)

            for p in range(2):
                act.wait_ge(s_xTout[p], 16 * (NT // 2 + (1 - p) + 1))
            load_xT(0)
            gate_hidden(0)
            gate_open(0)
            mix_turned(0)
            with act.Fori(0, NT) as i:
                act.wait_ge(s_v2, i + 1)
                act.dma_start(xin, x_t[:, bass.ds(i, 1), :].rearrange("p a c -> p (a c)")).then_inc(s_xin, 16)
                act.wait_ge(s_p, i + 1)
                load_xT(i + 1)
                gate_hidden(i + 1)
                act.wait_ge(s_v2, i + 2)
                act.activation(col["std"][:], mv[:, 1:2], ACT.Sqrt, bias=eps[:, 0:1]).then_inc(s_std2, 1)
                act.wait_ge(s_tx3, i + 1)
                act.activation(x3T, bank[3][:, C:C + KC * T].rearrange("p (k t) -> p k t", k=KC), ACT.Copy).then_inc(s_x3T, 1)
                gate_open(i + 1)
                hidden(i, 0)
                mix_turned(i + 1)
                hidden(i, 1)

        @block.tensor
        def _(pe):
            pe.wait_ge(s_setup, SETUP)
            pe.sem_inc(s_oh_free, GC)
            pe.sem_inc(s_slot_free, RING)
            pe.sem_inc(s_ekfree, 2)
            pe.wait_ge(s_edge_f, 2)
            for b in range(BL):
                if b >= 2:
                    pe.wait_ge(s_dstc, b - 1)
                    pe.wait_ge(s_srcc, b - 1)
                pe.transpose(bank[b % 2][:, 0:128], dst_f[:, b, :], ident[:]).then_inc(s_tr, 1)
                pe.transpose(bank[2 + b % 2][:, 0:128], src_f[:, b, :], ident[:]).then_inc(s_tr, 1)
            pe.wait_ge(s_dstc, BL)
            pe.wait_ge(s_last, 1)
            pe.wait_ge(s_lastrow, 1)
            pe.matmul(bank[4][0:NT + 1, 0:NG], last_row, dstT[:, 2 * GC - 1::GC], start=True, stop=True)
            pe.matmul(bank[5][0:NT + 1, 0:1], ones[:, 0:NT + 1], small[:, 0:1], start=True, stop=True).then_inc(s_lastb, 1)
            pe.wait_ge(s_bcol, 1)
            for c in range(3):
                m = pe.matmul(bank[6][0:1, c * (NT + 1):(c + 1) * (NT + 1)], bcol[:, c:c + 1], ident[0:NT + 1, 0:NT + 1],
                              start=True, stop=True)
            m.then_inc(s_brow, 1)
            pe.wait_ge(s_bounds, 1)
            pe.wait_ge(s_srcc, BL)

            def turn(t, p):
                pe.wait_ge(s_xn, t + 1)
                for k in range(KC):
                    m = pe.transpose(xT_psum(p)[:, k * T:(k + 1) * T], xn[:, p, k * 128:(k + 1) * 128], ident[0:T, 0:T])
                m.then_inc(s_xT, 1)

            turn(0, 0)
            pe.wait_ge(s_wA, 32)
            with pe.Fori(0, NT // BODY) as i:
                for s in range(BODY):
                    t = i * BODY + s
                    pe.wait_ge(s_xTc, t + 1)
                    if s % 2 == 0:
                        pe.wait_ge(s_sparse, (i * (BODY // 2) + s // 2 + 1) * 2)
                    for k in range(KC):
                        m = pe.matmul(h_psum(s), xT[:, s % 2, k * T:(k + 1) * T], w_neigh[:, k, :],
                                      start=(k == 0), stop=(k == KC - 1))
                    m.then_inc(s_h, 1)
                    turn(t + 1, (s + 1) % 2)
                    pe.wait_ge(s_kvc, t + 1)
                    for k in range(KC):
                        m = pe.matmul(bank[1 + s % 2][0:T, :], xT[:, s % 2, k * T:(k + 1) * T], wkv[:, k, :],
                                      start=(k == 0), stop=(k == KC - 1))
                    m.then_inc(s_kv, 1)
            pe.wait_ge(s_km, 1)
            for k in range(KC):
                m = pe.transpose(bank[0][:, k * T:(k + 1) * T], kmax[:, k * 128:(k + 1) * 128], ident[0:T, 0:T])
            m.then_inc(s_kmT, 1)
            pe.wait_ge(s_wC, 16)
            for h in range(KC):
                for k in range(KC):
                    m = pe.transpose(bank[6][:, h * C + k * 128:h * C + (k + 1) * 128],
                                     wq[:, k, h * 128:(h + 1) * 128], ident[:])
            m.then_inc(s_wqT, 1)
            pe.wait_ge(s_dg, 1)
            for k in range(KC):
                m = pe.matmul(bank[1][0:T, k * 128:(k + 1) * 128], ones[:, 0:T], kdiag[:, k, :], start=True, stop=True)
            m.then_inc(s_kmb, 1)
            pe.wait_ge(s_wprep, 1)
            for k in range(KC):
                pe.matmul(bank[4][0:T, 0:GH], ln_bT[:, k, :], wg1[:, k, :], start=(k == 0), stop=False)
            pe.matmul(bank[4][0:T, 0:GH], ones[0:1, 0:T], bg1_row[:], start=False, stop=True).then_inc(s_bg1, 1)
            pe.wait_ge(s_vones, 1)
            for h in range(KC):
                pe.matmul(bank[2 + h][:, 0:VH], zeros16[:, 0:128], zeros16[:, 0:VH], start=True, stop=False, skip_group_check=True)
            with pe.Fori(0, NT // 10) as i:
                for p in range(2):
                    pe.wait_ge(s_kexp, i * 2 + p + 1)
                    for b in range(5):
                        for h in range(KC):
                            m = pe.matmul(bank[2 + h][:, 0:VH], ek[:, p, b * C + h * 128:b * C + (h + 1) * 128],
                                          v_all[:, bass.ds(i * 10 + p * 5 + b, 1), h, :],
                                          start=False, stop=False, skip_group_check=True)
                    m.then_inc(s_ekfree, 1)
            for h in range(KC):
                m = pe.matmul(bank[2 + h][:, 0:VH], zeros16[:, 0:128], zeros16[:, 0:VH], start=False, stop=True, skip_group_check=True)
            m.then_inc(s_ctx, 1)
            pe.wait_ge(s_wqTc, 1)
            pe.wait_ge(s_bd, 1)
            for k in range(KC):
                for h in range(KC):
                    m = pe.matmul(bank[7][:, k * C + h * 128:k * C + (h + 1) * 128], wqT[:, h, k * 128:(k + 1) * 128],
                                  ctx_bd[:, h, :], start=True, stop=True)
            m.then_inc(s_wout, 1)
            pe.wait_ge(s_woutc, 1)
            pe.wait_ge(s_ready, 1)
            pe.wait_ge(s_wF, 16 * 7)

            def mix_first(j):
                pe.wait_ge(s_xTl, (j + 1) * 16)
                if not isinstance(j, int):
                    pe.wait_ge(s_mix, j)
                for k in range(KC):
                    pe.matmul(bank[2][0:T, 0:C], xTc[:, k, :], w_out[:, k, :], start=(k == 0), stop=(k == KC - 1))
                for k in range(KC):
                    m = pe.matmul(bank[2][0:T, C:C + GH], xTc[:, k, :], wg1g[:, k, :], start=(k == 0), stop=(k == KC - 1))
                m.then_inc(s_og, 1)

            def turn_gate(j):
                hold(pe, s_hg, j + 1)
                pe.transpose(bank[5][0:GH, C:C + T], hg, ident[0:T, 0:T]).then_inc(s_thg, 1)

            def gate_product(j):
                pe.wait_ge(s_hgT, j + 1)
                pe.matmul(bank[5][0:T, 0:C], hgT, wg2[:], start=True, stop=True).then_inc(s_g2, 1)

            def turn_mixed(j):
                pe.wait_ge(s_mix, j + 1)
                for k in range(KC):
                    m = pe.transpose(bank[3][:, k * T:(k + 1) * T], mixed[:, k * 128:(k + 1) * 128], ident[0:T, 0:T])
                m.then_inc(s_tm, 1)

            def project(j):
                pe.wait_ge(s_mixT, j + 1)
                for k in range(KC):
                    pe.matmul(bank[6][0:T, 0:C], xTc[:, k, :], w_self[:, k, :], start=(k == 0), stop=False)
                for k in range(KC):
                    m = pe.matmul(bank[6][0:T, 0:C], mixT[:, k, :], wproj[:, k, :], start=False, stop=(k == KC - 1))
                m.then_inc(s_p, 1)

            def turn_x3(i):
                pe.wait_ge(s_x3, i + 2)
                for k in range(KC):
                    m = pe.transpose(bank[3][:, C + k * T:C + (k + 1) * T], x3[:, k * 128:(k + 1) * 128], ident[0:T, 0:T])
                m.then_inc(s_tx3, 1)

            def ffn_up(i, half):
                pe.wait_ge(s_x3T, i + 1)
                for b in range(NH // 2):
                    n = half * (NH // 2) + b
                    for k in range(KC):
                        m = pe.matmul(bank[(7, 4)[half]][:, b * T:(b + 1) * T], w1[:, k, n * 128:(n + 1) * 128], x3T[:, k, :],
                                      start=(k == 0), stop=(k == KC - 1))
                m.then_inc((s_f1a, s_f1b)[half], 1)

            def ffn_down(i):
                pe.wait_ge(s_hidT, (i + 1) * 2)
                pe.wait_ge(s_deg, NT if isinstance(i, int) else i + 1)
                for n in range(NH):
                    m = pe.matmul(bank[1][0:T, C:2 * C], hidT[:, n, :], w2[:, n, :], start=(n == 0), stop=(n == NH - 1))
                m.then_inc(s_y, 1)

            def visit(t, g, release):
                pe.wait_ge(s_landed, g + 1)
                slot = pe.snap((g % RING) * GC)
                for s in range(GC):
                    pe.wait_ge(s_oh, (g + t) * GC + s + 1)
                    m = pe.matmul(bank[0][0:T, :], onehot[:, s, :], ring[:, bass.ds(slot + s, 1), :],
                                  start=False, stop=False, skip_group_check=True)
                    pe.matmul(bank[1][0:T, 0:2], onehot[:, s, :], ones16[:], start=False, stop=False,
                              skip_group_check=True).then_inc(s_oh_free, 1)
                if release:
                    m.then_inc(s_slot_free, 1)

            mix_first(0)
            turn_gate(0)
            gate_product(0)
            turn_mixed(0)
            project(0)
            with pe.Fori(0, NT) as i:
                g0 = pe.value_load(bounds[0:1, bass.ds(i, 1)], min_val=0, max_val=NG * NT)
                g1 = pe.value_load(bounds[0:1, bass.ds(i + 1, 1)], min_val=0, max_val=NG * NT)
                pe.wait_ge(s_x3, i + 1)
                pe.matmul(bank[0][0:T, :], zeros16[:, 0:T], zeros16[:], start=True, stop=False, skip_group_check=True)
                pe.matmul(bank[1][0:T, 0:2], zeros16[:, 0:T], zeros16[:, 0:2], start=True, stop=False, skip_group_check=True)
                with pe.If(g1 > g0):
                    with pe.Fori(g0, g1) as g:
                        visit(i, g, True)
                visit(i, g1, False)
                pe.matmul(bank[0][0:T, :], zeros16[:, 0:T], zeros16[:], start=False, stop=True, skip_group_check=True)
                pe.matmul(bank[1][0:T, 0:2], zeros16[:, 0:T], zeros16[:, 0:2], start=False, stop=True,
                          skip_group_check=True).then_inc(s_agg, 1)
                mix_first(i + 1)
                ffn_down(i)
                turn_gate(i + 1)
                turn_x3(i)
                gate_product(i + 1)
                ffn_up(i, 0)
                turn_mixed(i + 1)
                ffn_up(i, 1)
                project(i + 1)
            ffn_down(NT)
            pe.wait_ge(s_cnt, 1)
            pe.matmul(bank[0][0:T, 0:1], ones[0:T, 0:T], col["cnt"][:], start=True, stop=True).then_inc(s_tot, 1)
            with pe.Fori(0, ROUNDS_D) as i:
                pe.wait_ge(s_cnt, i + 2)
                pe.matmul(bank[0][0:T, 0:CANDS], ones[0:T, 0:T], counts[:, 0:CANDS], start=True, stop=True).then_inc(s_tot, 1)
            pe.wait_ge(s_cnt, ROUNDS_D + 2)
            pe.matmul(bank[0][0:T, 0:1], ones[0:T, 0:T], counts[:, 0:1], start=True, stop=True).then_inc(s_tot, 1)
            pe.wait_ge(s_cnt, ROUNDS_D + 3)
            pe.matmul(bank[0][0:T, 0:1], ones[0:T, 0:T], col["cnt"][:], start=True, stop=True)
            pe.matmul(bank[1][0:T, 0:NT], ones[0:T, 0:T], eqm, start=True, stop=True)
            pe.matmul(bank[2][0:T, 0:NT], upper[:], eqm, start=True, stop=True).then_inc(s_tot, 1)

        @block.vector
        def _(dve):
            dve.sem_inc(s_sparse, BODY)
            dve.sem_inc(s_v2, 1)
            dve.sem_inc(s_x3, 1)
            dve.wait_ge(s_edges, 16 * 9)
            st = Steps(dve, s_vec[0])
            dve.tensor_copy(dst_f, dst_raw).then_inc(s_edge_f, 1)
            dve.tensor_copy(src_f, src_raw).then_inc(s_edge_f, 1)
            a = st.mark(dve.tensor_tensor(falls, dst_raw, nxt_raw, ALU.is_gt))
            st.after(a)
            dve.tensor_reduce(small[:, 0:1], falls.rearrange("p a b -> p (a b)"), AX_X, ALU.add).then_inc(s_last, 1)
            dve.wait_ge(s_setup, SETUP)
            for b in range(BL):
                w = min(128, CH - b * 128)
                dve.wait_ge(s_tr, 2 * b + 1)
                dve.tensor_copy(dstT[:, GC + b * 128:GC + b * 128 + w], bank[b % 2][:, 0:w]).then_inc(s_dstc, 1)
                if b == 0:
                    dve.tensor_scalar(last_row, ones[:, 0:NT + 1], ident[:, 127:128], None, ALU.mult).then_inc(s_lastrow, 1)
            dve.wait_ge(s_lastb, 1)
            a = st.mark(dve.tensor_scalar(below, bank[4][0:NT + 1, 0:NG], tile_edge[:, 0:1], None, ALU.is_lt))
            b = st.mark(dve.tensor_scalar(small[0:NT + 1, 1:2], bank[5][0:NT + 1, 0:1], 1.0, None, ALU.min))
            c = st.mark(dve.tensor_scalar(small[0:NT + 1, 2:3], tile_flat[:], -1.0, 0.0, ALU.add, ALU.max))
            st.after(a)
            a = st.mark(dve.tensor_reduce(small[0:NT + 1, 3:4], below, AX_X, ALU.add))
            st.after(a)
            a = st.mark(dve.tensor_tensor(small[0:NT + 1, 4:5], small[0:NT + 1, 2:3], small[0:NT + 1, 3:4], ALU.subtract))
            st.after(a)
            dve.scalar_tensor_tensor(out=bcol[:, 0:1], in0=small[0:NT + 1, 4:5], scalar=small[0:NT + 1, 1:2],
                                     in1=small[0:NT + 1, 3:4], op0=ALU.mult, op1=ALU.add)
            dve.tensor_scalar(bcol[:, 1:2], tile_flat[:], small[0:NT + 1, 1:2], None, ALU.mult)
            dve.tensor_scalar(bcol[:, 2:3], small[0:NT + 1, 1:2], float(NT - 1), 1.0, ALU.mult, ALU.add).then_inc(s_bcol, 1)
            for c in range(5):
                dve.wait_ge(s_xload[c], 16)
                for t in range(c * XL, (c + 1) * XL):
                    dve.bn_stats(stats[:, t, :], x_all[:, t, 0:C]).then_inc(s_stats, 1)
            dve.wait_ge(s_brow, 1)
            dve.tensor_copy(bounds[:], bank[6][0:1, 0:3 * (NT + 1)]).then_inc(s_bounds, 1)
            dve.wait_ge(s_stats, NT)
            me, mo, ve, vo = (stats[:, :, n] for n in (1, 4, 2, 5))
            a = st.mark(dve.tensor_tensor(sums, me, mo, ALU.add))
            b = st.mark(dve.tensor_tensor(diff, me, mo, ALU.subtract))
            c = st.mark(dve.tensor_tensor(var2, ve, vo, ALU.add))
            st.after(a)
            a = st.mark(dve.tensor_scalar(mean, sums, 0.5, None, ALU.mult))
            st.after(c)
            b = st.mark(dve.tensor_tensor(var, diff, diff, ALU.mult))
            st.after(b)
            b = st.mark(dve.scalar_tensor_tensor(out=std1b, in0=var, scalar=C / 4.0, in1=var2, op0=ALU.mult, op1=ALU.add))
            st.after(b)
            dve.tensor_scalar(var, std1b, 1.0 / C, None, ALU.mult).then_inc(s_var, 1)
            dve.wait_ge(s_std, 1)
            a = st.mark(dve.reciprocal(rstd[:, 0:NT], std1))
            st.after(a)
            a = st.mark(dve.tensor_tensor(sums, var, rstd[:, 0:NT], ALU.mult))
            st.after(a)
            dve.tensor_tensor(var2, sums, rstd[:, 0:NT], ALU.mult).then_inc(s_var, 1)
            dve.scalar_tensor_tensor(out=shift[:, 0:NT], in0=mean, scalar=-1.0, in1=rstd[:, 0:NT],
                                     op0=ALU.mult, op1=ALU.mult).then_inc(s_norm, 1)
            dve.wait_ge(s_std, 2)
            dve.reciprocal(gate_scale[:, 0:NT], stdg).then_inc(s_gs, 1)
            dve.wait_ge(s_small, SMALL)
            for k in range(KC):
                dve.tensor_scalar(wg1g[:, k, :], wg1[:, k, :], ln_g[:, k:k + 1], None, ALU.mult)
                last = dve.tensor_scalar(ln_bT[:, k, :], ones[:, 0:T], ln_b[:, k:k + 1], None, ALU.mult)
            last.then_inc(s_wprep, 1)

            with dve.Fori(0, NT // BODY) as i:
                st = Steps(dve, s_vec[1], i * STEPS_A, s_alone)
                for pr in range(BODY // 2):
                    t = i * BODY + 2 * pr
                    hold(dve, s_h, t + 2)
                    done, found = [None, None], [None, None]
                    for k in range(TOPK // 8):
                        for u in range(2):
                            src = h_psum(2 * pr + u) if k == 0 else taken[:, u, :]
                            if k:
                                st.after(done[u])
                            found[u] = st.mark(dve.max(top8[:, u * (TOPK // 8) + k, :], src))
                        for u in range(2):
                            src = h_psum(2 * pr + u) if k == 0 else taken[:, u, :]
                            st.after(found[u])
                            done[u] = st.mark(dve.match_replace(out=taken[:, u, :], in_to_replace=top8[:, u * (TOPK // 8) + k, :],
                                                                in_values=src, imm_value=BELOW))
                    dve.wait_ge(s_split, t + 2)
                    for u in range(2):
                        st.after(done[u])
                        last = dve.scalar_tensor_tensor(out=sparse[:, u, :], in0=taken[:, u, :], scalar=BELOW,
                                                        in1=h_psum(2 * pr + u), op0=ALU.is_equal, op1=ALU.mult)
                        last.then_inc(s_sparse, 1)
                dve.wait_ge(s_kvc, (i + 1) * BODY + 2)
                dve.tensor_reduce(kparts[:, bass.ds(i, 1), :].rearrange("p a c -> p (a c)"),
                                  k_all[:, bass.ds(i * BODY, BODY), :].rearrange("p t c -> p c t"), AX_X, ALU.max)\
                   .then_inc(s_kpart, 1)
            assert st.n == STEPS_A, st.n
            st = Steps(dve, s_vec[2])
            dve.wait_ge(s_kpart, NT // BODY)
            dve.tensor_reduce(kmax, kparts.rearrange("p a c -> p c a"), AX_X, ALU.max).then_inc(s_km, 1)
            dve.memset(v_all[:, 0:NT, :, 128:VH], 1.0).then_inc(s_vones, 1)
            dve.wait_ge(s_kmT, 1)
            a = st.mark(dve.tensor_reduce(kmaxT[:], bank[0][:, 0:KC * T].rearrange("p (k t) -> p k t", k=KC), AX_X, ALU.max))
            st.after(a)
            for k in range(KC):
                last = dve.tensor_scalar(kdiag[:, k, :], ident[:], kmaxT[:, k:k + 1], None, ALU.mult)
            last.then_inc(s_dg, 1)
            dve.wait_ge(s_kmb, 1)
            a = st.mark(dve.tensor_copy(kmaxb, bank[1][0:T, 0:C]))
            st.after(a)
            with dve.Fori(0, NT // 5) as i:
                ks = k_all[:, bass.ds(i * 5, 5), :]
                dve.tensor_tensor(ks, ks, kmaxb.rearrange("p (a c) -> p a c", a=1).to_broadcast([T, 5, C]), ALU.subtract)\
                   .then_inc(s_ksub, 1)
            dve.wait_ge(s_bg1, 1)
            dve.tensor_copy(bg1[:], bank[4][0:T, 0:GH]).then_inc(s_bg1c, 1)
            dve.wait_ge(s_ctx, 1)
            for h in range(KC):
                a = st.mark(dve.reciprocal(ctx_r[:, h:h + 1], bank[2 + h][:, 128:129]))
            st.after(a)
            for h in range(KC):
                for b in range(128 // HD):
                    d = slice(b * HD, (b + 1) * HD)
                    last = dve.tensor_scalar(ctx_bd[d, h, d], bank[2 + h][d, d], ctx_r[d, h:h + 1], None, ALU.mult)
            last.then_inc(s_bd, 1)
            dve.memset(hidT, 0.0)
            dve.memset(hgT[GH:GH + 1, :], 1.0)
            dve.memset(ones_row, 1.0)
            dve.memset(tile_base[:], 0.0).then_inc(s_base, 1)
            dve.wait_ge(s_wF, 16 * 7)
            dve.wait_ge(s_bg1c, 1)
            dve.wait_ge(s_gs, 1)
            dve.tensor_scalar(wproj, wproj, 0.5, None, ALU.mult).then_inc(s_ready, 1)

            def gate_pre(j):
                dve.wait_ge(s_og, j + 1)
                dve.scalar_tensor_tensor(out=hg_pre, in0=bank[2][0:T, C:C + GH], scalar=gate_scale[:, bass.ds(j, 1)],
                                         in1=bg1[:], op0=ALU.mult, op1=ALU.add).then_inc(s_hgpre, 1)

            def mix(j):
                dve.wait_ge(s_gate, j + 1)
                dve.scalar_tensor_tensor(out=mixed, in0=gate, scalar=1.0, in1=bank[2][0:T, 0:C],
                                         op0=ALU.add, op1=ALU.mult).then_inc(s_mix, 1)

            def ffn_rows(st, i):
                dve.wait_ge(s_y, i + 1)
                a = st.mark(dve.tensor_tensor(ybias, bank[1][0:T, C:2 * C], b2, ALU.add))
                st.after(a)
                dve.tensor_scalar(yw_all[:, bass.ds(i, 1), :], ybias.rearrange("p (a c) -> p a c", a=1),
                                  w_all[:, bass.ds(i, 1)], None, ALU.mult).then_inc(s_yw, 1)

            def visit(t, g, base):
                at = nc.s_assert_within(dve.snap((g - base) * GC + GC), 0, CH,
                                        skip_runtime_bounds_check_because="g is in the pass over the edges that starts at base")
                for s in range(GC):
                    dve.wait_ge(s_oh_free, (g + t) * GC + s + 1)
                    dve.tensor_scalar(onehot[:, s, :], iota[:], tile_base[:, 0:1], dstT[:, bass.ds(at + s, 1)],
                                      ALU.add, ALU.is_equal).then_inc(s_oh, 1)

            gate_pre(0)
            mix(0)
            with dve.Fori(0, NT) as i:
                g0 = dve.value_load(bounds[0:1, bass.ds(i, 1)], min_val=0, max_val=NG * NT)
                g1 = dve.value_load(bounds[0:1, bass.ds(i + 1, 1)], min_val=0, max_val=NG * NT)
                base = dve.value_load(bounds[0:1, bass.ds(i + NT + 1, 1)], min_val=0, max_val=NG * NT)
                st = Steps(dve, s_vec[3], i * STEPS_C)
                hold(dve, s_base, i + 1)
                with dve.If(g1 > g0):
                    with dve.Fori(g0, g1) as g:
                        visit(i, g, base)
                visit(i, g1, base)
                dve.wait_ge(s_oh, (g1 + i + 1) * GC)
                dve.tensor_scalar(tile_base[:], tile_base[:], float(T), None, ALU.add).then_inc(s_base, 1)
                dve.wait_ge(s_bounds, 1)
                dve.wait_ge(s_xin, (i + 1) * 16)
                a = st.mark(dve.tensor_tensor(base_x, xin, bproj, ALU.add))
                dve.wait_ge(s_p, i + 1)
                st.after(a)
                a = st.mark(dve.tensor_tensor(base_p, base_x, bank[6][0:T, 0:C], ALU.add))
                dve.wait_ge(s_agg, i + 1)
                dve.tensor_scalar(col["deg"][:], bank[1][0:T, 0:1], 1.0, None, ALU.max).then_inc(s_deg, 1)
                c = st.mark(dve.tensor_copy(junk, bank[0][0:T, 0:C]))
                dve.wait_ge(s_deg, i + 1)
                b = st.mark(dve.reciprocal(col["rdeg"][:], col["deg"][:]))
                st.after(c)
                c = st.mark(dve.scalar_tensor_tensor(out=agg_sum, in0=bank[0][0:T, C:2 * C], scalar=1.0 / LO_SCALE,
                                                     in1=junk, op0=ALU.mult, op1=ALU.add))
                st.after(c)
                a = st.mark(dve.scalar_tensor_tensor(out=x2, in0=agg_sum, scalar=col["rdeg"][:, 0:1], in1=base_p,
                                                     op0=ALU.mult, op1=ALU.add))
                st.after(a)
                a = st.mark(dve.bn_stats(bn6[:], x2))
                hold(dve, s_vec[3], i * STEPS_C + a)
                a = st.mark(dve.bn_aggr(mv[:], bn6[:]))
                st.after(a)
                dve.sem_inc(s_v2, 1)
                gate_pre(i + 1)
                dve.wait_ge(s_std2, i + 1)
                a = st.mark(dve.reciprocal(col["rstd"][:], col["std"][:]))
                st.after(a)
                a = st.mark(dve.tensor_scalar(x3, x2, mv[:, 0:1], col["rstd"][:, 0:1], ALU.subtract, ALU.mult))
                st.after(a)
                dve.sem_inc(s_x3, 1)
                a = st.mark(dve.tensor_tensor_reduce(out=junk, in0=x3, in1=wr, scale=1.0, scalar=0.0, op0=ALU.mult,
                                                     op1=ALU.add, accum_out=col["w"][:]))
                dve.tensor_tensor(res_all[:, bass.ds(i, 1), :], x2.rearrange("p (a c) -> p a c", a=1),
                                  x3.rearrange("p (a c) -> p a c", a=1), ALU.add).then_inc(s_res, 1)
                st.after(a)
                a = st.mark(dve.tensor_scalar(w_all[:, bass.ds(i + 1, 1)], col["w"][:], br[:, 0:1], None, ALU.add))
                ffn_rows(st, i)
                st.after(a)
                mix(i + 1)
            assert st.n == STEPS_C, st.n
            st = Steps(dve, s_vec[4])
            ffn_rows(st, NT)
            w = w_all[:, 1:NT + 1]
            c = {n: col[n][:, 0:1] for n in col}
            dve.tensor_scalar(hit, w, 0.0, 0.0, ALU.is_ge, ALU.add, accum_out=c["cnt"]).then_inc(s_cnt, 1)
            dve.wait_ge(s_tot, 1)
            a = st.mark(dve.tensor_scalar(c["pos"], bank[0][0:T, 0:1], float(KEEP), None, ALU.is_ge))
            st.after(a)
            a = st.mark(dve.tensor_scalar(c["sgn"], c["pos"], 2.0, -1.0, ALU.mult, ALU.add))
            b = st.mark(dve.tensor_scalar(c["goal"], c["pos"], float(2 * KEEP - N - 1), float(N - KEEP + 1), ALU.mult, ALU.add))
            st.after(a)
            a = st.mark(dve.tensor_scalar(wv, w, c["sgn"], None, ALU.mult))
            top = 31 - DIGIT
            dve.memset(best[:], 0)
            for n in range(CANDS):
                dve.memset(cand[:, n:n + 1], (n + 1) << top)
                b = st.mark(dve.memset(digits[:, n:n + 1], (n + 1) << top))
            b = st.mark(dve.memset(c["bit"], float(1 << top)))
            st.after(b)

            def count(n):
                return dve.tensor_scalar(hit_n[:, n, :], wv, cand[:, n:n + 1].bitcast(F32), 0.0, ALU.is_ge, ALU.add,
                                         accum_out=counts[:, n:n + 1])

            base0 = st.n
            with dve.Fori(0, ROUNDS_D) as i:
                st = Steps(dve, s_vec[4], i * STEPS_D + base0)
                for n in range(CANDS):
                    last = count(n)
                last.then_inc(s_cnt, 1)
                a = st.mark(dve.tensor_scalar(digits, digits, DIGIT, None, ALU.logical_shift_right))
                dve.wait_ge(s_tot, i + 2)
                b = st.mark(dve.tensor_scalar(over[:, 0:CANDS], bank[0][0:T, 0:CANDS], c["goal"], 0.0, ALU.is_ge, ALU.add,
                                              accum_out=c["pos"]))
                st.after(b)
                b = st.mark(dve.tensor_scalar(accept[:], c["pos"], c["bit"], None, ALU.mult))
                st.after(b)
                b = st.mark(dve.tensor_tensor(best[:], best[:], accept[:], ALU.bitwise_or))
                a = st.mark(dve.tensor_scalar(c["bit"], c["bit"], 1.0 / 2 ** DIGIT, None, ALU.mult))
                st.after(b)
                b = st.mark(dve.tensor_tensor(cand[:, 0:CANDS], best[:].to_broadcast([T, CANDS]), digits[:, 0:CANDS], ALU.bitwise_or))
                st.after(b)
                b = st.mark(dve.memset(accept[:], 1))
                st.after(b)
            assert st.n == STEPS_D, st.n
            st = Steps(dve, s_vec[4], base0 + ROUNDS_D * STEPS_D)
            a = st.mark(dve.tensor_tensor(cand[:, 0:1], best[:], accept[:], ALU.bitwise_or))
            st.after(a)
            count(0).then_inc(s_cnt, 1)
            dve.wait_ge(s_tot, ROUNDS_D + 2)
            a = st.mark(dve.tensor_scalar(accept[:], bank[0][0:T, 0:1], c["goal"], None, ALU.is_ge))
            st.after(a)
            a = st.mark(dve.tensor_tensor(best[:], best[:], accept[:], ALU.bitwise_or))
            st.after(a)
            a = st.mark(dve.tensor_scalar(c["thr"], best[:].bitcast(F32), c["sgn"], None, ALU.mult))
            st.after(a)
            a = st.mark(dve.tensor_scalar(gtm, w, c["thr"], 0.0, ALU.is_gt, ALU.add, accum_out=c["cnt"]))
            b = st.mark(dve.tensor_scalar(eqm, w, c["thr"], None, ALU.is_equal))
            st.after(b)
            dve.sem_inc(s_cnt, 1)
            dve.wait_ge(s_tot, ROUNDS_D + 3)
            a = st.mark(dve.tensor_scalar(c["need"], bank[0][0:T, 0:1], -1.0, float(KEEP), ALU.mult, ALU.add))
            b = st.mark(dve.tensor_tensor_scan(colcum, ones_row, bank[1][0:T, 0:NT], 0.0, ALU.mult, ALU.add))
            st.after(b)
            b = st.mark(dve.tensor_tensor(colcum, colcum, bank[1][0:T, 0:NT], ALU.subtract))
            st.after(b)
            b = st.mark(dve.tensor_tensor(prefix, colcum, bank[2][0:T, 0:NT], ALU.add))
            st.after(b)
            b = st.mark(dve.scalar_tensor_tensor(out=hit, in0=prefix, scalar=c["need"], in1=eqm, op0=ALU.is_lt, op1=ALU.mult))
            st.after(b)
            b = st.mark(dve.tensor_tensor(selm, hit, gtm, ALU.add))
            st.after(b)
            dve.wait_ge(s_yw, NT + 1)
            dve.wait_ge(s_res, NT)
            for t in range(NT):
                dve.scalar_tensor_tensor(out=res_all[:, t, :], in0=yw_all[:, t + 1, :], scalar=selm[:, t:t + 1],
                                         in1=res_all[:, t, :], op0=ALU.mult, op1=ALU.add).then_inc(s_fin, 1)


_INS = ["x", "src", "dst", "L0_gnn_W_self", "L0_gnn_W_neigh", "L0_mix_Wqkv", "L0_mix_Wproj", "L0_mix_bproj",
        "L0_mix_ln_g", "L0_mix_ln_b", "L0_mix_Wg1", "L0_mix_bg1", "L0_mix_Wg2", "L0_mix_bg2",
        "L0_ffn_attention_mask", "L0_ffn_wr", "L0_ffn_br", "L0_ffn_w1", "L0_ffn_b1", "L0_ffn_w2", "L0_ffn_b2"]


def kernel(**inputs):
    import numpy as _np
    import concourse.bacc as _bacc
    from concourse import mybir as _mybir
    from concourse.bass_utils import run_bass_kernel_spmd as _run

    nc = _bacc.Bacc("TRN2", target_bir_lowering=False, num_devices=1)
    arrays, args = {}, []
    for name in _INS:
        a = _np.ascontiguousarray(inputs[name])
        arrays[f"in_{name}_dram"] = a
        args.append(nc.dram_tensor(f"in_{name}_dram", a.shape, _mybir.dt.from_np(a.dtype), kind="ExternalInput").ap())
    out = nc.dram_tensor("out_dram", inputs["x"].shape, _mybir.dt.float32, kind="ExternalOutput").ap()
    build(nc, *args, out)
    r = _run(nc, [arrays], core_ids=[0])
    return r.results[0]["out_dram"]
```

```python
from contextlib import ExitStack

import concourse.bass as bass
from concourse import mybir

F32 = mybir.dt.float32
F16 = mybir.dt.float16
I32 = mybir.dt.int32
ALU = mybir.AluOpType
ACT = mybir.ActivationFunctionType
AX_X = mybir.AxisListType.X

EPS = 1e-5
TOPK = 32
BELOW = -3.0e38
NOWHERE = 1 << 20
LO_SCALE = 4096.0


class Steps:

    def __init__(self, engine, semaphore, base=0, alone=None):
        self.engine, self.semaphore, self.base, self.alone, self.n = engine, semaphore, base, alone, 0

    def mark(self, instruction):
        instruction.then_inc(self.semaphore, 1)
        self.n += 1
        return self.n

    def after(self, n):
        self.engine.wait_ge(self.semaphore, self.base + n)
        if self.alone is not None:
            self.engine.sem_inc(self.alone, 1)


def build(nc, x_d, src_d, dst_d, w_self_d, w_neigh_d, wqkv_d, wproj_d, bproj_d, ln_g_d, ln_b_d, wg1_d, bg1_d,
          wg2_d, bg2_d, mask_d, wr_d, br_d, w1_d, b1_d, w2_d, b2_d, out_d):
    N, C = x_d.shape
    E = src_d.shape[0]
    T = 125
    NT = N // T
    KC = C // 128
    GH = wg1_d.shape[1]
    HID = w1_d.shape[1]
    NH = HID // 128
    HD = 32
    KEEP = N // 2 - 1
    BODY = 10
    assert NT * T == N and NT % BODY == 0 and C == 256

    CHUNK = 128
    GC = 4
    RING = 8
    ROUNDS = -(-E // (CHUNK * GC * RING))
    NG = ROUNDS * RING
    CH = NG * GC
    assert (NG - 1) * GC * CHUNK >= E
    FULL = E // CHUNK
    REST = E - FULL * CHUNK
    BL = -(-(FULL + 1) // 128)
    TAIL = FULL - (BL - 1) * 128
    XL = NT // 5

    ND = 1
    PER = 14
    UNROLL = 12
    REST_AT = ND * PER
    WIN = 10
    NW = -(-T // WIN)
    KEYS = NT * WIN
    PAIR = 2
    NPAIR = CH // PAIR
    SHARE = [1] * 13 + [0]
    assert sum(SHARE) == NW and len(SHARE) == PER and KEYS <= 512 and PER % 2 == 0
    assert (NT - REST_AT) % UNROLL == 0 and UNROLL % 2 == 0
    HL = 5
    DEG_MAX = 24 * CHUNK
    FAR_MAX = 512
    assert 2 * 2049 - DEG_MAX - CHUNK > FAR_MAX
    T_G0, T_G1, T_FIRST, T_VIS, T_WIN = 0, NT, 2 * NT, 3 * NT, 4 * NT
    T_PASSES = T_WIN + ND * NW + 1
    T_ROUNDS, T_START, T_DENSE, T_GENERAL, T_END = (T_PASSES + n for n in range(1, 6))
    NEDGE = ND * NW + 1

    with ExitStack() as ctx:
        def sb(name, shape, dt=F32):
            return ctx.enter_context(nc.sbuf_tensor(name, shape, dt))

        def sem(name):
            return ctx.enter_context(nc.semaphore(name))

        s_alone = sem("s_alone")

        def hold(engine, semaphore, value):
            engine.wait_ge(semaphore, value)
            engine.sem_inc(s_alone, 1)

        class Region:

            def __init__(self, name, words):
                self.mem, self.at, self.words = sb(name, [128, words]), 0, words

            def take(self, shape, dt=F32):
                n = 1
                for s in shape[1:]:
                    n *= s
                words = n // 2 if dt == F16 else n
                assert self.at + words <= self.words
                ap = self.mem[0:shape[0], self.at:self.at + words]
                self.at += words
                if dt != F32:
                    ap = ap.bitcast(dt)
                if len(shape) == 3:
                    ap = ap.rearrange("p (a b) -> p a b", a=shape[1])
                if len(shape) == 4:
                    ap = ap.rearrange("p (a b c) -> p a b c", a=shape[1], b=shape[2])
                return ap

        region_k = Region("region_k", NT * C)
        dst_raw = region_k.take([128, BL, 128], I32)
        nxt_raw = region_k.take([128, BL, 128], I32)
        src_raw = region_k.take([128, BL, 128], I32)
        dst_f = region_k.take([128, BL, 128])
        src_f = region_k.take([128, BL, 128])
        falls = region_k.take([128, BL, 128])
        same_dst = region_k.take([128, FULL])
        same_src = falls.rearrange("p a b -> p (a b)")[:, 0:FULL]
        region_k.at = 0
        keys = region_k.take([128, CH])
        src_lo = region_k.take([128, CH])
        counts16 = region_k.take([T, NT, T + 1], F16)[:, :, 0:T]
        hs = region_k.take([T, HL, HL * 2 * C], F16)
        k_all = region_k.mem[0:T, 0:NT * C].rearrange("p (t c) -> p t c", c=C)
        yw_all = k_all

        VH = 130
        VW = KC * VH
        region_v = Region("region_v", (NT + 2) * VW)
        x_all = region_v.mem[0:T, :].rearrange("p (t w) -> p t w", w=VW)
        v_all = region_v.mem[0:T, :].rearrange("p (t h w) -> p t h w", h=KC, w=VH)
        w1 = region_v.take([128, KC, HID])
        w2 = region_v.take([128, NH, C])
        w_self = region_v.take([128, KC, C])
        wproj = region_v.take([128, KC, C])
        w_out = region_v.take([128, KC, C])
        b2 = region_v.take([T, C])
        bproj = region_v.take([T, C])
        wr = region_v.take([T, C])
        xin = region_v.take([T, C])
        agg_sum = region_v.take([T, C])
        base_x = region_v.take([T, C])
        base_p = region_v.take([T, C])
        x2 = region_v.take([T, C])
        x3 = region_v.take([T, C])
        gate = region_v.take([T, C])
        mixed = region_v.take([T, C])
        ybias = region_v.take([T, C])
        junk = region_v.take([T, C])
        mixT = region_v.take([128, KC, T])
        x3T = region_v.take([128, KC, T])
        xTc = region_v.take([128, KC, T])
        hidT = region_v.take([128, NH, T])
        hgT = region_v.take([GH + 1, T])
        hg_pre = region_v.take([T, GH])
        hg = region_v.take([T, GH])
        wv = region_v.take([T, NT])
        hit = region_v.take([T, NT])
        hit_n = region_v.take([T, 7, NT])
        eqm = region_v.take([T, NT])
        gtm = region_v.take([T, NT])
        selm = region_v.take([T, NT])
        colcum = region_v.take([T, NT])
        ones_row = region_v.take([T, NT])
        prefix = region_v.take([T, NT])
        yw = region_v.take([T, 2, C])
        scaled = [region_v.take([T, 1]) for _ in range(3)]
        root, square, halved = region_v.take([T, 1]), region_v.take([T, 1]), region_v.take([T, 1], I32)
        lo_hot = region_v.take([128, PAIR, 126], F16)[:, :, 0:T]
        key_hot = region_v.take([128, PAIR, KEYS], F16)
        cand = region_v.take([T, 8], I32)
        digits = region_v.take([T, 8], I32)
        counts = region_v.take([T, 8])
        over = region_v.take([T, 8])

        region_r = Region("region_r", NT * C)
        res_all = region_r.mem[0:T, :].rearrange("p (t c) -> p t c", c=C)
        w_neigh = region_r.take([128, KC, C])
        wkv = region_r.take([128, KC, 2 * C])
        wq = region_r.take([128, KC, C])
        wqT = region_r.take([128, KC, C])
        kdiag = region_r.take([128, KC, 128])
        ek_at = region_r.at
        ek = region_r.take([T, 2, 5 * C])
        region_r.at, after_ek = ek_at, region_r.at
        win_below = region_r.take([NEDGE, NPAIR])
        row_b = region_r.take([1, NT + 1])
        row_w = region_r.take([1, NEDGE])
        edge_row = region_r.take([1, ND + 1, NW])
        sorted_t = region_r.take([1, 4 * NT])
        general_t = region_r.take([1, 4 * NT])
        misc = region_r.take([1, 8])
        start_i = region_r.take([1, 1], I32)
        assert region_r.at <= after_ek
        region_r.at = after_ek
        xn = region_r.take([T, 2, C])
        xT = region_r.take([128, 2, KC * T])
        at = region_r.at
        src_lo_r, keys_r = region_r.take([128, CH]), region_r.take([128, CH])
        region_r.at = at
        taken = region_r.take([T, 2, C])
        sparse = region_r.take([T, 2, C])
        rest32 = region_r.take([T, C])
        split16 = region_r.take([T, 2, 2 * C], F16)
        top8 = region_r.take([T, 2 * (TOPK // 8), 8])
        kparts = region_r.take([T, NT // BODY, C])
        kmax = region_r.take([T, C])
        kmaxb = region_r.take([T, C])
        stats = region_r.take([T, NT, 6])
        mean = region_r.take([T, NT])
        var = region_r.take([T, NT])
        sums = region_r.take([T, NT])
        diff = region_r.take([T, NT])
        var2 = region_r.take([T, NT])
        std1 = region_r.take([T, NT])
        std1b = region_r.take([T, NT])
        stdg = region_r.take([T, NT])
        below = region_r.take([NT + 1, NG])
        last_row = region_r.take([128, max(NT + 1, NEDGE)])
        ln_bT = region_r.take([128, KC, T])
        wg1 = region_r.take([128, KC, GH])

        ring = sb("ring", [128, RING * GC, 2 * C], F16)
        dstT = sb("dstT", [128, GC + CH])
        srcT = sb("srcT", [128, CH + GC], I32)
        stage = sb("stage", [128, RING * GC], I32)
        bounds = sb("bounds", [1, T_END], I32)
        ident = sb("ident", [128, 128])
        ones = sb("ones", [128, 128])
        upper = sb("upper", [T, T])
        iota = sb("iota", [128, 2 * C], F16)
        tile_start = sb("tile_start", [128, NT])
        win_start = sb("win_start", [128, ND, NW])
        zeros16 = sb("zeros16", [128, VH], F16)
        ones16 = sb("ones16", [128, 2], F16)
        onehot = sb("onehot", [128, GC, T], F16)
        rstd = sb("rstd", [T, NT + 2])
        shift = sb("shift", [T, NT + 2])
        gate_scale = sb("gate_scale", [T, NT + 2])
        kmaxT = sb("kmaxT", [128, KC])
        ctx_bd = sb("ctx_bd", [128, KC, 128])
        ctx_r = sb("ctx_r", [128, KC])
        wg1g = sb("wg1g", [128, KC, GH])
        wg2 = sb("wg2", [GH + 1, C])
        bg1 = sb("bg1", [T, GH])
        bg1_row = sb("bg1_row", [1, GH])
        ln_g = sb("ln_g", [128, KC])
        ln_b = sb("ln_b", [128, KC])
        br = sb("br", [T, 1])
        b1 = sb("b1", [128, NH])
        eps = sb("eps", [T, 1])
        w_all = sb("w_all", [T, NT])
        w_at = sb("w_at", [T, NT + 2])
        small = sb("small", [128, 16])
        tile_edge = sb("tile_edge", [NT + 1, 1])
        bcol = sb("bcol", [max(NT + 1, NEDGE), 2])
        bn6 = sb("bn6", [T, 6])
        mv = sb("mv", [T, 2])
        col = {n: sb("col_" + n, [T, 1]) for n in (
            "rstd", "deg", "rdeg", "w", "cnt", "pos", "sgn", "goal", "bit", "thr", "need")}
        best = sb("best", [T, 1], I32)
        accept = sb("accept", [T, 1], I32)

        bank = [ctx.enter_context(nc.psum_tensor(f"bank{i}", [128, 512], F32)) for i in range(8)]
        rows_d = nc.dram_tensor("rows_d", (N, 2 * C), F16).ap()
        yw_d = nc.dram_tensor("yw_d", (NT, T, C), F32).ap()
        xT_d = nc.dram_tensor("xT_d", (NT + 1, 128, KC * T), F32).ap()

        s_const, s_setup, s_edges, s_small = sem("s_const"), sem("s_setup"), sem("s_edges"), sem("s_small")
        s_wB, s_wrap = sem("s_wB"), sem("s_wrap")
        s_xload = [sem(f"s_xload{i}") for i in range(5)]
        s_wA, s_wC, s_wF = sem("s_wA"), sem("s_wC"), sem("s_wF")
        s_pool = sem("s_pool")
        s_vec = [sem(f"s_vec{i}") for i in range(5)]
        s_edge_f, s_tr, s_dstc, s_srcc = sem("s_edge_f"), sem("s_tr"), sem("s_dstc"), sem("s_srcc")
        s_last, s_lastb, s_bcol, s_brow, s_bounds = sem("s_last"), sem("s_lastb"), sem("s_bcol"), sem("s_brow"), sem("s_bounds")
        s_var, s_std, s_norm = sem("s_var"), sem("s_std"), sem("s_norm")
        s_xn, s_xT, s_xTc, s_h, s_kv, s_kvc, s_km = (sem(n) for n in ("s_xn", "s_xT", "s_xTc", "s_h", "s_kv", "s_kvc", "s_km"))
        s_vones = sem("s_vones")
        s_sparse, s_split = sem("s_sparse"), sem("s_split")
        s_xTout = [sem("s_xTout0"), sem("s_xTout1")]
        s_rows = [sem("s_rows0"), sem("s_rows1")]
        s_kmT, s_dg, s_kmb, s_ksub, s_kexp, s_ekfree = (sem(n) for n in ("s_kmT", "s_dg", "s_kmb", "s_ksub", "s_kexp", "s_ekfree"))
        s_ctx, s_bd, s_wqT, s_wqTc, s_wout, s_woutc = (sem(n) for n in ("s_ctx", "s_bd", "s_wqT", "s_wqTc", "s_wout", "s_woutc"))
        s_wprep, s_bg1, s_ready = sem("s_wprep"), sem("s_bg1"), sem("s_ready")
        s_land = [sem(f"s_land{i}") for i in range(RING * GC)]
        s_landed, s_slot_free, s_stage = sem("s_landed"), sem("s_slot_free"), sem("s_stage")
        s_oh, s_oh_free, s_agg = sem("s_oh"), sem("s_oh_free"), sem("s_agg")
        s_xin, s_xTl, s_og, s_hgpre, s_hg, s_thg, s_hgT = (
            sem(n) for n in ("s_xin", "s_xTl", "s_og", "s_hgpre", "s_hg", "s_thg", "s_hgT"))
        s_g2, s_gate, s_mix, s_tm, s_mixT, s_p = (sem(n) for n in ("s_g2", "s_gate", "s_mix", "s_tm", "s_mixT", "s_p"))
        s_deg, s_v2, s_x3, s_tx3, s_x3T = (sem(n) for n in ("s_deg", "s_v2", "s_x3", "s_tx3", "s_x3T"))
        s_f1a, s_f1b, s_hidT, s_y, s_yw = (sem(n) for n in ("s_f1a", "s_f1b", "s_hidT", "s_y", "s_yw"))
        s_cnt, s_tot, s_fin, s_res = sem("s_cnt"), sem("s_tot"), sem("s_fin"), sem("s_res")
        s_lastrow, s_stats, s_gs, s_kpart, s_bg1c = (sem(n) for n in ("s_lastrow", "s_stats", "s_gs", "s_kpart", "s_bg1c"))
        s_out = sem("s_out")
        s_ywout, s_ywin = [sem("s_ywout0"), sem("s_ywout1")], sem("s_ywin")
        s_lag = sem("s_lag")
        s_hot, s_hot_free, s_counts, s_evac = (sem(n) for n in ("s_hot", "s_hot_free", "s_counts", "s_evac"))
        s_hload, s_hfree = [sem(f"s_hload{n}") for n in range(HL)], sem("s_hfree")

        x_t = x_d.rearrange("(t p) c -> p t c", p=T)
        out_t = out_d.rearrange("(t p) c -> p t c", p=T)
        rows_t = rows_d.rearrange("(t p) c -> p t c", p=T)
        xT_t = xT_d.rearrange("t p w -> p t w")
        yw_t = yw_d.rearrange("t p c -> p t c")
        SMALL = 8 * 16
        SETUP = 23
        DIGIT = 3
        ROUNDS_D = 10
        CANDS = 2 ** DIGIT - 1
        STEPS_A = (BODY // 2) * 2 * 2 * (TOPK // 8)
        STEPS_C = 25
        STEPS_D = 6

        def tile_at(i, s):
            return i if s == PER - 1 else i * (PER - 1) + s + ND

        def next_tile(i, s):
            return tile_at(i, s + 1) if s + 1 < PER else tile_at(i + 1, 0)

        def positions(engine, position):
            with engine.Fori(0, ND) as i:
                k = 0
                for s in range(PER):
                    position(i * PER + s, tile_at(i, s), next_tile(i, s), s % 2, i * (PER // 2) + s // 2,
                             i, range(k, k + SHARE[s]), s == PER - 1, s, s == PER - 1)
                    k += SHARE[s]
            with engine.Fori(0, (NT - REST_AT) // UNROLL) as j:
                for u in range(UNROLL):
                    n = j * UNROLL + (REST_AT + u)
                    position(n, n, n + 1, u % 2, j * (UNROLL // 2) + (REST_AT + u) // 2, None, range(0), False,
                             u, u == UNROLL - 1)

        def load(engine, at, low=0, high=NG * NT + NG):
            return engine.value_load(bounds[0:1, bass.ds(at, 1)], min_val=low, max_val=high)

        class Ends:

            def __init__(self, engine):
                self.engine, self.end, self.ahead, self.visits = engine, None, None, None

            def enter(self, n, s):
                if s == 0:
                    self.end, self.visits = load(self.engine, n), load(self.engine, n + T_VIS)
                    self.ahead = load(self.engine, n + T_G1)
                g0, self.end = self.end, self.ahead
                return g0, self.end, self.visits + s

            def look_ahead(self, n, last):
                if not last:
                    self.ahead = load(self.engine, n + 1 + T_G1)

        def count_bank(k):
            return bank[(7, 4)[k % 2]]

        def h_psum(s):
            return bank[3 + s // 2][0:T, (s % 2) * C:(s % 2 + 1) * C]

        def xT_psum(s):
            return bank[0][:, (s % 2) * C:(s % 2) * C + KC * T]

        block = ctx.enter_context(nc.Block())

        @block.sync
        def _(sp):
            for p in range(2):
                sp.sem_inc(s_rows[p], 16)
                sp.sem_inc(s_xTout[p], 16)
            sp.wait_ge(s_const, 4)
            full = (BL - 1) * 128 * 128
            for raw, d, o in ((dst_raw, dst_d, 0), (nxt_raw, dst_d, 1), (src_raw, src_d, 0)):
                sp.dma_start(raw[:, 0:BL - 1, :],
                             d[o:o + full].rearrange("(b r e) -> r b e", r=128, e=128)).then_inc(s_edges, 16)
                sp.dma_start(raw[0:TAIL, BL - 1, :],
                             d[full + o:full + o + TAIL * 128].rearrange("(r e) -> r e", e=128)).then_inc(s_edges, 16)
                sp.dma_start(raw[TAIL:TAIL + 1, BL - 1, 0:REST - o],
                             d[full + o + TAIL * 128:E].rearrange("(a e) -> a e", a=1)).then_inc(s_edges, 16)
            for i in range(5):
                sp.dma_start(x_all[:, i * XL:(i + 1) * XL, 0:C], x_t[:, i * XL:(i + 1) * XL, :]).then_inc(s_xload[i], 16)
            sp.dma_start(w_neigh, w_neigh_d.rearrange("(k p) n -> p k n", p=128)).then_inc(s_wA, 16)
            sp.dma_start(wkv, wqkv_d[:, C:3 * C].rearrange("(k p) n -> p k n", p=128)).then_inc(s_wA, 16)
            sp.dma_start(wq, wqkv_d[:, 0:C].rearrange("(k p) n -> p k n", p=128)).then_inc(s_wC, 16)
            with sp.Fori(0, NT // 2) as i:
                for p in range(2):
                    sp.wait_ge(s_split, i * 2 + p + 1 + 2)
                    sp.dma_start(rows_t[:, bass.ds(i * 2 + p, 1), :], split16[:, p:p + 1, :]).then_inc(s_rows[p], 16)
            sp.wait_ge(s_ctx, 1)
            for dst, src in ((w_self, w_self_d.rearrange("(k p) n -> p k n", p=128)),
                             (wproj, wproj_d.rearrange("(k p) n -> p k n", p=128)),
                             (bproj, bproj_d.partition_broadcast(T)),
                             (b2, b2_d.partition_broadcast(T)),
                             (wr, wr_d.rearrange("n a -> (n a)").partition_broadcast(T))):
                sp.dma_start(dst, src).then_inc(s_wF, 16)
            sp.dma_start(w1, w1_d.rearrange("(k p) n -> p k n", p=128)).then_inc(s_wB, 16)
            sp.dma_start(w2, w2_d.rearrange("(k p) n -> p k n", p=128)).then_inc(s_wB, 16)
            sp.wait_ge(s_bounds, 1)
            passes = load(sp, T_PASSES, 1, NT)
            rounds = load(sp, T_ROUNDS, 1, ROUNDS)
            with sp.Fori(0, passes) as r:
                with sp.Fori(0, rounds) as j:
                    for q in range(RING):
                        for s in range(GC):
                            sp.wait_ge(s_land[q * GC + s], (r * ROUNDS + j + 1) * 16)
                        sp.sem_inc(s_landed, 1)
            for p in range(2):
                sp.wait_ge(s_ywout[p], 16 * (NT // 2 + 1))
            for i in range(ND):
                tile, n = tile_at(i, 0), i * PER
                sp.dma_start(yw_all[:, tile:tile + PER - 1, :], yw_t[:, n + 2:n + PER + 1, :]).then_inc(s_ywin, 16)
                sp.dma_start(yw_all[:, i:i + 1, :], yw_t[:, n + PER + 1:n + PER + 2, :]).then_inc(s_ywin, 16)
            sp.dma_start(yw_all[:, REST_AT:NT - 2, :], yw_t[:, REST_AT + 2:NT, :]).then_inc(s_ywin, 16)
            for i in range(5):
                sp.wait_ge(s_fin, XL * (i + 1))
                sp.dma_start(out_t[:, i * XL:(i + 1) * XL, :], res_all[:, i * XL:(i + 1) * XL, :]).then_inc(s_out, 16)
            sp.wait_ge(s_out, 16 * 5)

        @block.gpsimd
        def _(pool):
            pool.sem_inc(s_split, 2)
            pool.memset(dst_raw[:, BL - 1, :], NOWHERE).then_inc(s_const, 1)
            pool.memset(nxt_raw[:, BL - 1, :], NOWHERE).then_inc(s_const, 1)
            pool.memset(src_raw[:, BL - 1, :], 0).then_inc(s_const, 1)
            pool.memset(x_all[:, NT:NT + 2, :], 0.0).then_inc(s_const, 1)
            for dst, src in ((ln_g[:], ln_g_d.rearrange("(k p) -> p k", p=128)),
                             (ln_b[:], ln_b_d.rearrange("(k p) -> p k", p=128)),
                             (b1[:], b1_d.rearrange("(k p) -> p k", p=128)),
                             (wg1, wg1_d.rearrange("(k p) n -> p k n", p=128)),
                             (wg2[0:GH, :], wg2_d),
                             (wg2[GH:GH + 1, :], bg2_d.rearrange("(a n) -> a n", a=1)),
                             (bg1_row[:], bg1_d.rearrange("(a n) -> a n", a=1)),
                             (br[:], br_d.partition_broadcast(T))):
                with nc.allow_non_contiguous_dma(reason="a few hundred words, once"):
                    pool.dma_start(dst, src).then_inc(s_small, 16)
            pool.memset(ident[:], 0.0).then_inc(s_pool, 1)
            pool.memset(upper[:], 1.0).then_inc(s_pool, 1)
            pool.wait_ge(s_pool, 2)
            pool.affine_select(out=ident[:], in_=ident[:], compare_op=ALU.not_equal, fill=1.0, base=0,
                               pattern=[[-1, 128]], channel_multiplier=1).then_inc(s_setup, 1)
            pool.affine_select(out=upper[:], in_=upper[:], compare_op=ALU.is_gt, fill=0.0, base=0,
                               pattern=[[1, T]], channel_multiplier=-1).then_inc(s_setup, 1)
            pool.iota(iota[:], [[1, 2 * C]], base=0, channel_multiplier=0,
                      allow_small_or_imprecise_dtypes=True).then_inc(s_setup, 1)
            pool.iota(tile_edge[:], [[0, 1]], base=0, channel_multiplier=T,
                      allow_small_or_imprecise_dtypes=True).then_inc(s_setup, 1)
            for ap, pattern, first in ((edge_row, [[T, ND + 1], [WIN, NW]], 0),
                                       (tile_start[:], [[T, NT]], 0),
                                       (win_start[:], [[T * NT, ND], [KEYS, NW]], 0),
                                       (general_t[:, 0:NT], [[NG, NT]], -1),
                                       (general_t[:, NT:2 * NT], [[NG, NT]], NG - 1),
                                       (general_t[:, T_FIRST:T_FIRST + NT], [[0, NT]], 0),
                                       (general_t[:, 3 * NT:4 * NT], [[1, NT]], 0),
                                       (sorted_t[:, T_VIS:T_VIS + REST_AT], [[PER - 1, ND], [1, PER]], 0),
                                       (sorted_t[:, T_VIS + REST_AT:T_VIS + NT], [[1, NT - REST_AT]], REST_AT - ND)):
                pool.iota(ap, pattern, base=first, channel_multiplier=0,
                          allow_small_or_imprecise_dtypes=True).then_inc(s_setup, 1)
            for ap, value in ((ones[:], 1.0), (zeros16[:], 0.0), (ones16[:], 1.0), (eps[:], EPS), (w_at[:], 0.0),
                              (gate_scale[:], 1.0), (rstd[:], 1.0), (shift[:], 0.0), (ctx_bd[:], 0.0),
                              (dstT[:, 0:GC], float(NOWHERE))):
                pool.memset(ap, value).then_inc(s_setup, 1)
            with pool.Fori(0, NT // 2) as i:
                for p in range(2):
                    t = i * 2 + p
                    pool.wait_ge(s_sparse, t + 1 + BODY)
                    hold(pool, s_rows[p], (i + 1) * 16)
                    st = Steps(pool, s_pool, t * 2 + 2, s_alone)
                    a = st.mark(pool.tensor_copy(split16[:, p, 0:C], sparse[:, p, :]))
                    st.after(a)
                    a = st.mark(pool.tensor_tensor(rest32, sparse[:, p, :], split16[:, p, 0:C], ALU.subtract))
                    st.after(a)
                    pool.tensor_scalar(split16[:, p, C:2 * C], rest32, LO_SCALE, None, ALU.mult).then_inc(s_split, 1)
            for p in range(2):
                pool.wait_ge(s_rows[p], 16 * (NT // 2 + 1))
            pool.wait_ge(s_srcc, BL)
            pool.tensor_copy(srcT[:, CH:], srcT[:, 0:GC]).then_inc(s_wrap, 1)
            pool.wait_ge(s_wrap, 1)
            pool.wait_ge(s_bounds, 1)
            passes = load(pool, T_PASSES, 1, NT)
            rounds = load(pool, T_ROUNDS, 1, ROUNDS)
            start = load(pool, T_START, 0, ROUNDS - 1)
            pool.wait_ge(s_slot_free, 1)
            pool.tensor_copy(stage[:, 0:GC], srcT[:, bass.ds(start * (RING * GC), GC)]).then_inc(s_stage, 1)
            with pool.Fori(0, passes) as r:
                with pool.Fori(0, rounds) as j:
                    for q in range(RING):
                        g = (r * ROUNDS + j) * RING + q
                        hold(pool, s_slot_free, g + 2)
                        nx = (q + 1) % RING * GC
                        at = nc.s_assert_within(pool.snap(((j + start) * RING + q + 1) * GC), 0, CH,
                                                skip_runtime_bounds_check_because="start + rounds is ROUNDS at most")
                        pool.tensor_copy(stage[:, nx:nx + GC], srcT[:, bass.ds(at, GC)]).then_inc(s_stage, 1)
                        hold(pool, s_stage, g + 1)
                        for s in range(GC):
                            c = q * GC + s
                            pool.indirect_dma_start(
                                out=ring[:, c, :], out_offset=None, in_=rows_d,
                                in_offset=bass.IndirectOffsetOnAxis(ap=stage[:, c:c + 1], axis=0)).then_inc(s_land[c], 16)

        @block.scalar
        def _(act):
            act.sem_inc(s_evac, 2)
            for b in range(BL):
                w = min(128, CH - b * 128)
                act.wait_ge(s_tr, 2 * b + 2)
                act.activation(srcT[:, b * 128:b * 128 + w], bank[2 + b % 2][:, 0:w], ACT.Copy).then_inc(s_srcc, 1)
            act.wait_ge(s_setup, SETUP)
            act.wait_ge(s_var, 1)
            act.activation(std1, var, ACT.Sqrt, bias=eps[:, 0:1]).then_inc(s_std, 1)
            act.wait_ge(s_var, 2)
            act.activation(stdg, var2, ACT.Sqrt, bias=eps[:, 0:1]).then_inc(s_std, 1)
            act.wait_ge(s_norm, 1)

            def normalise(t, p):
                act.activation(xn[:, p, :].rearrange("p (a c) -> p a c", a=1), x_all[:, bass.ds(t, 1), 0:C], ACT.Identity,
                               bias=shift[:, bass.ds(t, 1)], scale=rstd[:, bass.ds(t, 1)]).then_inc(s_xn, 1)

            def keep_xT(t, p):
                act.wait_ge(s_xT, t + 1)
                act.activation(xT[:, p, :], xT_psum(p), ACT.Copy).then_inc(s_xTc, 1)

            def store_xT(t, p):
                act.wait_ge(s_xTc, t + 1)
                act.dma_start(xT_t[:, bass.ds(t, 1), :], xT[:, p:p + 1, :]).then_inc(s_xTout[p], 16)

            normalise(0, 0)
            keep_xT(0, 0)
            normalise(1, 1)
            store_xT(0, 0)
            act.sem_inc(s_kvc, 2)
            with act.Fori(0, NT // BODY) as i:
                for s in range(BODY):
                    t, p = i * BODY + s, (s + 1) % 2
                    act.wait_ge(s_xTout[p], (i * (BODY // 2) + (s + 1) // 2 + 1) * 16)
                    keep_xT(t + 1, p)
                    normalise(t + 2, s % 2)
                    store_xT(t + 1, p)
                    act.wait_ge(s_kv, t + 1)
                    kv = bank[1 + s % 2]
                    act.activation(k_all[:, bass.ds(t, 1), :], kv[0:T, 0:C].rearrange("p (a c) -> p a c", a=1), ACT.Copy)
                    act.activation(v_all[:, bass.ds(t, 1), :, 0:128],
                                   kv[0:T, C:2 * C].rearrange("p (a h c) -> p a h c", a=1, h=KC), ACT.Copy).then_inc(s_kvc, 1)
            with act.Fori(0, NT // 10) as i:
                for p in range(2):
                    act.wait_ge(s_ksub, i * 2 + p + 1)
                    act.wait_ge(s_ekfree, i * 2 + p + 1)
                    act.activation(ek[:, p, :], region_k.mem[0:T, bass.ds((i * 2 + p) * (5 * C), 5 * C)], ACT.Exp).then_inc(s_kexp, 1)
            act.wait_ge(s_wqT, 1)
            act.activation(wqT, bank[6][:, :].rearrange("p (k c) -> p k c", k=KC), ACT.Copy).then_inc(s_wqTc, 1)
            act.wait_ge(s_wout, 1)
            act.activation(w_out, bank[7][:, :].rearrange("p (k c) -> p k c", k=KC), ACT.Copy).then_inc(s_woutc, 1)
            act.wait_ge(s_ready, 1)

            def load_xT(j, tile):
                act.dma_start(xTc.rearrange("p k t -> p (k t)"), xT_t[:, bass.ds(tile, 1), :].rearrange("p a w -> p (a w)"))\
                   .then_inc(s_xTl, 16)

            def gate_hidden(j):
                act.wait_ge(s_hgpre, j + 1)
                act.activation(hg, hg_pre, ACT.Gelu).then_inc(s_hg, 1)

            def gate_turned(j):
                act.wait_ge(s_thg, j + 1)
                act.activation(hgT[0:GH, :], bank[5][0:GH, C:C + T], ACT.Copy).then_inc(s_hgT, 1)

            def gate_open(j):
                act.wait_ge(s_g2, j + 1)
                act.activation(gate, bank[5][0:T, 0:C], ACT.Tanh, scale=0.5).then_inc(s_gate, 1)

            def mix_turned(j):
                act.wait_ge(s_tm, j + 1)
                act.activation(mixT, bank[3][:, 0:KC * T].rearrange("p (k t) -> p k t", k=KC), ACT.Copy).then_inc(s_mixT, 1)

            def keep_x3T(i):
                act.wait_ge(s_tx3, i + 1)
                act.activation(x3T, bank[3][:, C:C + KC * T].rearrange("p (k t) -> p k t", k=KC), ACT.Copy).then_inc(s_x3T, 1)

            def hidden(i, half):
                act.wait_ge((s_f1a, s_f1b)[half], i + 1)
                for b in range(NH // 2):
                    n = half * (NH // 2) + b
                    last = act.activation(hidT[:, n, :], bank[(7, 4)[half]][:, b * T:(b + 1) * T],
                                          ACT.Gelu_apprx_tanh, bias=b1[:, n:n + 1])
                last.then_inc(s_hidT, 1)

            for p in range(2):
                act.wait_ge(s_xTout[p], 16 * (NT // 2 + (1 - p) + 1))
            load_xT(0, tile_at(0, 0))
            gate_hidden(0)
            gate_turned(0)
            gate_open(0)
            mix_turned(0)
            def load_h(part):
                act.dma_start(hs[:, part % HL, :].rearrange("p (b c) -> p b c", b=HL),
                              rows_t[:, part * HL:(part + 1) * HL, :]).then_inc(s_hload[part % HL], 16)

            dense = load(act, T_DENSE, 0, 1)
            with act.If(dense > 0):
                for part in range(HL):
                    load_h(part)
            def position(n, tile, after, u, half, i, windows, from_counts, s, last):
                act.wait_ge(s_v2, n + 1)
                act.dma_start(xin, x_t[:, bass.ds(tile, 1), :].rearrange("p a c -> p (a c)")).then_inc(s_xin, 16)
                act.wait_ge(s_p, n + 1)
                load_xT(n + 1, after)
                for k in windows:
                    act.wait_ge(s_counts, i * NW + k + 1)
                    wide = min(WIN, T - k * WIN)
                    act.activation(counts16[:, :, k * WIN:k * WIN + wide],
                                   count_bank(k)[0:T, 0:KEYS].rearrange("p (d h) -> p h d", h=NT)[:, :, 0:wide],
                                   ACT.Copy).then_inc(s_evac, 1)
                if from_counts:
                    with act.If(dense > 0):
                        for part in range(HL, 2 * HL):
                            act.wait_ge(s_hfree, i * (2 * HL) + part - HL + 1)
                            load_h(part)
                        with act.If(i < ND - 1):
                            for part in range(HL):
                                act.wait_ge(s_hfree, i * (2 * HL) + HL + part + 1)
                                load_h(part)
                keep_x3T(n)
                gate_hidden(n + 1)
                hidden(n, 0)
                gate_turned(n + 1)
                hidden(n, 1)
                gate_open(n + 1)
                mix_turned(n + 1)
                act.wait_ge(s_yw, n + 2)
                act.dma_start(yw_t[:, bass.ds(n, 1), :], yw[:, u:u + 1, :]).then_inc(s_ywout[u], 16)

            positions(act, position)
            keep_x3T(NT)
            hidden(NT, 0)
            hidden(NT, 1)

        @block.tensor
        def _(pe):
            pe.wait_ge(s_setup, SETUP)
            pe.sem_inc(s_oh_free, GC)
            pe.sem_inc(s_slot_free, RING)
            pe.sem_inc(s_ekfree, 2)
            pe.sem_inc(s_hot_free, PAIR)
            pe.wait_ge(s_edge_f, 2)
            for b in range(BL):
                if b >= 2:
                    pe.wait_ge(s_dstc, b - 1)
                    pe.wait_ge(s_srcc, b - 1)
                pe.transpose(bank[b % 2][:, 0:128], dst_f[:, b, :], ident[:]).then_inc(s_tr, 1)
                pe.transpose(bank[2 + b % 2][:, 0:128], src_f[:, b, :], ident[:]).then_inc(s_tr, 1)
            pe.wait_ge(s_dstc, BL)
            pe.wait_ge(s_last, 1)
            pe.wait_ge(s_lastrow, 1)
            pe.wait_ge(s_lag, 2)
            pe.matmul(bank[4][0:NT + 1, 0:NG], last_row[:, 0:NT + 1], dstT[:, 2 * GC - 1::GC], start=True, stop=True)
            for h in range(2):
                first = GC + PAIR - 1 + h * (CH // 2)
                pe.matmul(bank[(5, 7)[h]][0:NEDGE, 0:NPAIR // 2], last_row[:, 0:NEDGE], dstT[:, first:first + CH // 2 - 1:PAIR],
                          start=True, stop=True)
            pe.matmul(bank[6][0:NEDGE, 0:1], edge_row.rearrange("p a b -> p (a b)")[:, 0:NEDGE], ones[0:1, 0:1],
                      start=True, stop=True)
            pe.matmul(bank[6][0:NT + 1, 1:4], ones[:, 0:NT + 1], small[:, 8:11], start=True, stop=True).then_inc(s_lastb, 1)
            pe.wait_ge(s_bcol, 1)
            pe.matmul(bank[6][0:1, 64:64 + NT + 1], bcol[0:NT + 1, 0:1], ident[0:NT + 1, 0:NT + 1], start=True, stop=True)
            pe.matmul(bank[6][0:1, 128:128 + NEDGE], bcol[0:NEDGE, 1:2], ident[0:NEDGE, 0:NEDGE], start=True, stop=True)\
              .then_inc(s_brow, 1)
            pe.wait_ge(s_bounds, 1)
            pe.wait_ge(s_srcc, BL)

            def turn(t, p):
                pe.wait_ge(s_xn, t + 1)
                for k in range(KC):
                    m = pe.transpose(xT_psum(p)[:, k * T:(k + 1) * T], xn[:, p, k * 128:(k + 1) * 128], ident[0:T, 0:T])
                m.then_inc(s_xT, 1)

            turn(0, 0)
            pe.wait_ge(s_wA, 32)
            with pe.Fori(0, NT // BODY) as i:
                for s in range(BODY):
                    t = i * BODY + s
                    pe.wait_ge(s_xTc, t + 1)
                    if s % 2 == 0:
                        pe.wait_ge(s_sparse, (i * (BODY // 2) + s // 2 + 1) * 2)
                    for k in range(KC):
                        m = pe.matmul(h_psum(s), xT[:, s % 2, k * T:(k + 1) * T], w_neigh[:, k, :],
                                      start=(k == 0), stop=(k == KC - 1))
                    m.then_inc(s_h, 1)
                    turn(t + 1, (s + 1) % 2)
                    pe.wait_ge(s_kvc, t + 1)
                    for k in range(KC):
                        m = pe.matmul(bank[1 + s % 2][0:T, :], xT[:, s % 2, k * T:(k + 1) * T], wkv[:, k, :],
                                      start=(k == 0), stop=(k == KC - 1))
                    m.then_inc(s_kv, 1)
            pe.wait_ge(s_km, 1)
            for k in range(KC):
                m = pe.transpose(bank[0][:, k * T:(k + 1) * T], kmax[:, k * 128:(k + 1) * 128], ident[0:T, 0:T])
            m.then_inc(s_kmT, 1)
            pe.wait_ge(s_wC, 16)
            for h in range(KC):
                for k in range(KC):
                    m = pe.transpose(bank[6][:, h * C + k * 128:h * C + (k + 1) * 128],
                                     wq[:, k, h * 128:(h + 1) * 128], ident[:])
            m.then_inc(s_wqT, 1)
            pe.wait_ge(s_dg, 1)
            for k in range(KC):
                m = pe.matmul(bank[1][0:T, k * 128:(k + 1) * 128], ones[:, 0:T], kdiag[:, k, :], start=True, stop=True)
            m.then_inc(s_kmb, 1)
            pe.wait_ge(s_wprep, 1)
            for k in range(KC):
                pe.matmul(bank[4][0:T, 0:GH], ln_bT[:, k, :], wg1[:, k, :], start=(k == 0), stop=False)
            pe.matmul(bank[4][0:T, 0:GH], ones[0:1, 0:T], bg1_row[:], start=False, stop=True).then_inc(s_bg1, 1)
            pe.wait_ge(s_vones, 1)
            for h in range(KC):
                pe.matmul(bank[2 + h][:, 0:VH], zeros16[:, 0:128], zeros16[:, 0:VH], start=True, stop=False, skip_group_check=True)
            with pe.Fori(0, NT // 10) as i:
                for p in range(2):
                    pe.wait_ge(s_kexp, i * 2 + p + 1)
                    for b in range(5):
                        for h in range(KC):
                            m = pe.matmul(bank[2 + h][:, 0:VH], ek[:, p, b * C + h * 128:b * C + (h + 1) * 128],
                                          v_all[:, bass.ds(i * 10 + p * 5 + b, 1), h, :],
                                          start=False, stop=False, skip_group_check=True)
                    m.then_inc(s_ekfree, 1)
            for h in range(KC):
                m = pe.matmul(bank[2 + h][:, 0:VH], zeros16[:, 0:128], zeros16[:, 0:VH], start=False, stop=True, skip_group_check=True)
            m.then_inc(s_ctx, 1)
            pe.wait_ge(s_wqTc, 1)
            pe.wait_ge(s_bd, 1)
            for k in range(KC):
                for h in range(KC):
                    m = pe.matmul(bank[7][:, k * C + h * 128:k * C + (h + 1) * 128], wqT[:, h, k * 128:(k + 1) * 128],
                                  ctx_bd[:, h, :], start=True, stop=True)
            m.then_inc(s_wout, 1)
            pe.wait_ge(s_woutc, 1)
            pe.wait_ge(s_ready, 1)
            pe.wait_ge(s_wF, 16 * 5)

            def mix_first(j):
                pe.wait_ge(s_xTl, (j + 1) * 16)
                if not (isinstance(j, int) and j == 0):
                    pe.wait_ge(s_mix, j)
                for k in range(KC):
                    pe.matmul(bank[2][0:T, 0:C], xTc[:, k, :], w_out[:, k, :], start=(k == 0), stop=(k == KC - 1))
                for k in range(KC):
                    m = pe.matmul(bank[2][0:T, C:C + GH], xTc[:, k, :], wg1g[:, k, :], start=(k == 0), stop=(k == KC - 1))
                m.then_inc(s_og, 1)

            def turn_gate(j):
                hold(pe, s_hg, j + 1)
                pe.transpose(bank[5][0:GH, C:C + T], hg, ident[0:T, 0:T]).then_inc(s_thg, 1)

            def gate_product(j):
                pe.wait_ge(s_hgT, j + 1)
                pe.matmul(bank[5][0:T, 0:C], hgT, wg2[:], start=True, stop=True).then_inc(s_g2, 1)

            def turn_mixed(j):
                pe.wait_ge(s_mix, j + 1)
                for k in range(KC):
                    m = pe.transpose(bank[3][:, k * T:(k + 1) * T], mixed[:, k * 128:(k + 1) * 128], ident[0:T, 0:T])
                m.then_inc(s_tm, 1)

            def project_self(j):
                for k in range(KC):
                    pe.matmul(bank[6][0:T, 0:C], xTc[:, k, :], w_self[:, k, :], start=(k == 0), stop=False)

            def project_mixed(j):
                pe.wait_ge(s_mixT, j + 1)
                for k in range(KC):
                    m = pe.matmul(bank[6][0:T, 0:C], mixT[:, k, :], wproj[:, k, :], start=False, stop=(k == KC - 1))
                m.then_inc(s_p, 1)

            def turn_x3(i):
                pe.wait_ge(s_x3, i + 1)
                for k in range(KC):
                    m = pe.transpose(bank[3][:, C + k * T:C + (k + 1) * T], x3[:, k * 128:(k + 1) * 128], ident[0:T, 0:T])
                m.then_inc(s_tx3, 1)

            def ffn_up(i, half):
                pe.wait_ge(s_x3T, i + 1)
                pe.wait_ge(s_wB, 16 * 2)
                for b in range(NH // 2):
                    n = half * (NH // 2) + b
                    for k in range(KC):
                        m = pe.matmul(bank[(7, 4)[half]][:, b * T:(b + 1) * T], w1[:, k, n * 128:(n + 1) * 128], x3T[:, k, :],
                                      start=(k == 0), stop=(k == KC - 1))
                m.then_inc((s_f1a, s_f1b)[half], 1)

            def ffn_down(i):
                pe.wait_ge(s_hidT, (i + 1) * 2)
                for n in range(NH):
                    m = pe.matmul(bank[6][0:T, C:2 * C], hidT[:, n, :], w2[:, n, :], start=(n == 0), stop=(n == NH - 1))
                m.then_inc(s_y, 1)

            def count_window(i, k, part):
                w = i * NW + k
                pairs0 = load(pe, w + T_WIN, 0, NPAIR)
                pairs1 = load(pe, w + (T_WIN + 1), 0, NPAIR)
                out = count_bank(k)[0:T, 0:KEYS]
                middle = None if part is None else pe.snap((pairs0 + pairs1) // 2)

                def count(c):
                    visited = pe.snap((c + w) * PAIR)
                    for u in range(PAIR):
                        pe.wait_ge(s_hot, visited + (u + 1))
                        pe.matmul(out, lo_hot[:, u, :], key_hot[:, u, :], start=False, stop=False,
                                  skip_group_check=True).then_inc(s_hot_free, 1)

                if part != 1:
                    pe.wait_ge(s_evac, w + max(k + 1, 2) - k)
                    pe.matmul(out, zeros16[:, 0:T], iota[:, 0:KEYS], start=True, stop=False, skip_group_check=True)
                if part == 0:
                    with pe.If(middle > pairs0):
                        with pe.Fori(pairs0, middle) as c:
                            count(c)
                    return
                with pe.Fori(middle if part == 1 else pairs0, pairs1 + 1) as c:
                    count(c)
                pe.matmul(out, zeros16[:, 0:T], iota[:, 0:KEYS], start=False, stop=True, skip_group_check=True)\
                  .then_inc(s_counts, 1)

            def visit(t, g, release):
                pe.wait_ge(s_landed, g + 1)
                slot = pe.snap((g % RING) * GC)
                visited = pe.snap((g + t) * GC)
                for s in range(GC):
                    pe.wait_ge(s_oh, visited + (s + 1))
                    m = pe.matmul(bank[0][0:T, :], onehot[:, s, :], ring[:, bass.ds(slot + s, 1), :],
                                  start=False, stop=False, skip_group_check=True)
                    pe.matmul(bank[1][0:T, 0:2], onehot[:, s, :], ones16[:], start=False, stop=False,
                              skip_group_check=True).then_inc(s_oh_free, 1)
                if release:
                    m.then_inc(s_slot_free, 1)

            mix_first(0)
            turn_gate(0)
            gate_product(0)
            turn_mixed(0)
            pe.matmul(bank[6][0:T, C:2 * C], zeros16[:, 0:T], iota[:, 0:C], start=True, stop=True).then_inc(s_y, 1)
            project_self(0)
            project_mixed(0)
            ends = Ends(pe)
            dense = load(pe, T_DENSE, 0, 1)
            general = load(pe, T_GENERAL, 0, 1)
            def position(n, tile, after, u, half, i, windows, from_counts, s, last):
                g0, g1, finals = ends.enter(n, s)

                def gathered():
                    cuts, parts = [g0], [part for k in windows for part in ([(k, 0), (k, 1)] if k == 0 else [(k, None)])]
                    if parts:
                        cuts.append(pe.snap((g0 + g1) // 2))
                    if len(parts) > 1:
                        cuts.insert(1, pe.snap((g0 + cuts[1]) // 2))
                    cuts.append(g1)
                    for at, (first, end) in enumerate(zip(cuts, cuts[1:])):
                        with pe.If(end > first):
                            with pe.Fori(first, end) as g:
                                visit(finals, g, True)
                        if at < len(parts):
                            count_window(i, *parts[at])
                    visit(finals, g1, False)

                pe.wait_ge(s_x3, n + 1)
                pe.matmul(bank[0][0:T, :], zeros16[:, 0:T], iota[:], start=True, stop=False, skip_group_check=True)
                pe.matmul(bank[1][0:T, 0:2], zeros16[:, 0:T], zeros16[:, 0:2], start=True, stop=False, skip_group_check=True)
                if not from_counts:
                    gathered()
                else:
                    pe.wait_ge(s_evac, (i + 1) * NW + 2)
                    with pe.If(dense > 0):
                        for part in range(2 * HL):
                            pe.wait_ge(s_hload[part % HL], (i * 2 + part // HL + 1) * 16)
                            for b in range(HL):
                                m = pe.matmul(bank[0][0:T, :], counts16[:, part * HL + b, :],
                                              hs[:, part % HL, b * 2 * C:(b + 1) * 2 * C],
                                              start=False, stop=False, skip_group_check=True)
                                if b == HL - 1:
                                    m.then_inc(s_hfree, 1)
                                pe.matmul(bank[1][0:T, 0:2], counts16[:, part * HL + b, :], ones16[0:T, :],
                                          start=False, stop=False, skip_group_check=True)
                    with pe.If(general > 0):
                        gathered()
                pe.matmul(bank[0][0:T, :], zeros16[:, 0:T], iota[:], start=False, stop=True, skip_group_check=True)
                pe.matmul(bank[1][0:T, 0:2], zeros16[:, 0:T], zeros16[:, 0:2], start=False, stop=True,
                          skip_group_check=True).then_inc(s_agg, 1)
                turn_x3(n)
                mix_first(n + 1)
                if len(windows):
                    pe.wait_ge(s_evac, i * NW + (windows[-1] + 1 + 2))
                ffn_up(n, 0)
                turn_gate(n + 1)
                ffn_up(n, 1)
                gate_product(n + 1)
                ends.look_ahead(n, last)
                ffn_down(n)
                turn_mixed(n + 1)
                project_self(n + 1)
                project_mixed(n + 1)

            positions(pe, position)
            pe.wait_ge(s_cnt, 1)
            pe.matmul(bank[0][0:T, 0:1], ones[0:T, 0:T], col["cnt"][:], start=True, stop=True).then_inc(s_tot, 1)
            turn_x3(NT)
            ffn_up(NT, 0)
            ffn_up(NT, 1)
            with pe.Fori(0, ROUNDS_D) as i:
                pe.wait_ge(s_cnt, i + 2)
                pe.matmul(bank[0][0:T, 0:CANDS], ones[0:T, 0:T], counts[:, 0:CANDS], start=True, stop=True).then_inc(s_tot, 1)
            pe.wait_ge(s_cnt, ROUNDS_D + 2)
            pe.matmul(bank[0][0:T, 0:1], ones[0:T, 0:T], counts[:, 0:1], start=True, stop=True).then_inc(s_tot, 1)
            pe.wait_ge(s_cnt, ROUNDS_D + 3)
            pe.matmul(bank[0][0:T, 0:1], ones[0:T, 0:T], col["cnt"][:], start=True, stop=True)
            pe.matmul(bank[1][0:T, 0:NT], ones[0:T, 0:T], eqm, start=True, stop=True)
            pe.matmul(bank[2][0:T, 0:NT], upper[:], eqm, start=True, stop=True).then_inc(s_tot, 1)
            pe.wait_ge(s_yw, NT + 2)
            ffn_down(NT)

        @block.vector
        def _(dve):
            dve.sem_inc(s_sparse, BODY)
            dve.sem_inc(s_v2, 1)
            dve.sem_inc(s_yw, 1)
            for p in range(2):
                dve.sem_inc(s_ywout[p], 16)
            dve.wait_ge(s_edges, 16 * 9)
            st = Steps(dve, s_vec[0])
            dve.tensor_copy(dst_f, dst_raw).then_inc(s_edge_f, 1)
            dve.tensor_copy(src_f, src_raw).then_inc(s_edge_f, 1)
            a = st.mark(dve.tensor_tensor(falls, dst_raw, nxt_raw, ALU.is_gt))
            st.after(a)
            dve.tensor_reduce(small[:, 8:9], falls.rearrange("p a b -> p (a b)"), AX_X, ALU.add).then_inc(s_last, 1)
            dve.wait_ge(s_setup, SETUP)
            for b in range(BL):
                w = min(128, CH - b * 128)
                dve.wait_ge(s_tr, 2 * b + 1)
                dve.tensor_copy(dstT[:, GC + b * 128:GC + b * 128 + w], bank[b % 2][:, 0:w]).then_inc(s_dstc, 1)
                if b == 0:
                    dve.tensor_scalar(last_row, ones[:, 0:max(NT + 1, NEDGE)], ident[:, 127:128], None, ALU.mult).then_inc(s_lastrow, 1)
            dve.wait_ge(s_dstc, BL)
            far = DEG_MAX // CHUNK
            dve.wait_ge(s_last, 1)
            a = st.mark(dve.tensor_tensor(same_dst[:, 0:FULL + 1 - far], dstT[:, GC:GC + FULL + 1 - far],
                                          dstT[:, GC + far:GC + FULL + 1], ALU.is_equal))
            st.after(a)
            dve.tensor_reduce(small[:, 9:10], same_dst[:, 0:FULL + 1 - far], AX_X, ALU.add).then_inc(s_lag, 1)
            dve.wait_ge(s_srcc, BL)
            dve.wait_ge(s_lag, 1)
            a = st.mark(dve.tensor_tensor(same_dst, dstT[:, GC:GC + FULL], dstT[:, GC + 1:GC + FULL + 1], ALU.is_equal))
            b = st.mark(dve.tensor_tensor(same_src, srcT[:, 0:FULL], srcT[:, 1:FULL + 1], ALU.is_equal))
            st.after(b)
            b = st.mark(dve.tensor_tensor(same_src, same_src, same_dst, ALU.mult))
            st.after(b)
            dve.tensor_reduce(small[:, 10:11], same_src, AX_X, ALU.add).then_inc(s_lag, 1)
            for c in range(5):
                dve.wait_ge(s_xload[c], 16)
                for t in range(c * XL, (c + 1) * XL):
                    dve.bn_stats(stats[:, t, :], x_all[:, t, 0:C]).then_inc(s_stats, 1)
            dve.wait_ge(s_lastb, 1)
            a = st.mark(dve.tensor_scalar(below, bank[4][0:NT + 1, 0:NG], tile_edge[:, 0:1], None, ALU.is_lt))
            b = st.mark(dve.tensor_copy(small[0:NEDGE, 4:5], bank[6][0:NEDGE, 0:1]))
            c = st.mark(dve.tensor_scalar(small[0:NT + 1, 5:6], bank[6][0:NT + 1, 3:4], -float(FAR_MAX), 0.0, ALU.add, ALU.max))
            st.after(c)
            for h in range(2):
                b = st.mark(dve.tensor_scalar(win_below[:, h * (NPAIR // 2):(h + 1) * (NPAIR // 2)],
                                              bank[(5, 7)[h]][0:NEDGE, 0:NPAIR // 2], small[0:NEDGE, 4:5], None, ALU.is_lt))
            d = st.mark(dve.tensor_scalar(small[0:NT + 1, 6:7], bank[6][0:NT + 1, 1:2], small[0:NT + 1, 5:6], None, ALU.add))
            st.after(d)
            d = st.mark(dve.tensor_tensor(small[0:NT + 1, 7:8], small[0:NT + 1, 6:7], bank[6][0:NT + 1, 2:3], ALU.add))
            st.after(d)
            d = st.mark(dve.tensor_scalar(small[0:NT + 1, 1:2], small[0:NT + 1, 7:8], 1.0, None, ALU.min))
            st.after(d)
            dve.tensor_reduce(bcol[0:NT + 1, 0:1], below, AX_X, ALU.add)
            dve.tensor_reduce(bcol[0:NEDGE, 1:2], win_below, AX_X, ALU.add).then_inc(s_bcol, 1)
            dve.wait_ge(s_brow, 1)
            general = small[0:1, 1:2]
            a = st.mark(dve.tensor_copy(row_b, bank[6][0:1, 64:64 + NT + 1]))
            b = st.mark(dve.tensor_copy(row_w, bank[6][0:1, 128:128 + NEDGE]))
            c = st.mark(dve.tensor_scalar(misc[:, 0:1], general, -1.0, 1.0, ALU.mult, ALU.add))
            d = st.mark(dve.memset(sorted_t[:, 0:3 * NT], 0.0))
            st.after(d)
            a = st.mark(dve.tensor_copy(start_i, row_b[:, ND:ND + 1]))
            st.after(a)
            a = st.mark(dve.tensor_scalar(start_i, start_i, RING.bit_length() - 1, None, ALU.logical_shift_right))
            st.after(a)
            a = st.mark(dve.tensor_copy(misc[:, 1:2], start_i))
            st.after(a)
            a = st.mark(dve.tensor_scalar(misc[:, 2:3], misc[:, 1:2], float(RING), None, ALU.mult))
            b = st.mark(dve.tensor_scalar(misc[:, 3:4], misc[:, 1:2], misc[:, 0:1], None, ALU.mult))
            st.after(a)

            for first, o in ((T_G0, 0), (T_G1, 1)):
                dve.tensor_scalar(sorted_t[:, first:first + REST_AT].rearrange("p (i s) -> p i s", s=PER)[:, :, 0:PER - 1],
                                  row_b[:, ND + o:REST_AT + o].rearrange("p (i s) -> p i s", s=PER - 1),
                                  misc[:, 2:3], None, ALU.subtract)
                a = st.mark(dve.tensor_scalar(sorted_t[:, first + REST_AT:first + NT], row_b[:, REST_AT + o:NT + o],
                                              misc[:, 2:3], None, ALU.subtract))
            a = st.mark(dve.tensor_scalar(sorted_t[:, T_FIRST:T_FIRST + 1], misc[:, 2:3], 1.0, None, ALU.mult))
            b = st.mark(dve.tensor_scalar(general_t, general_t, 0.0, None, ALU.max))
            st.after(a)
            a = st.mark(dve.memset(sorted_t[:, 0:1], 0.0))
            st.after(a)
            a = st.mark(dve.tensor_tensor(general_t, general_t, sorted_t, ALU.subtract))
            st.after(a)
            dve.scalar_tensor_tensor(out=bounds[:, 0:4 * NT], in0=general_t, scalar=general, in1=sorted_t, op0=ALU.mult, op1=ALU.add)
            dve.tensor_scalar(bounds[:, T_WIN:T_WIN + NEDGE], row_w, misc[:, 0:1], None, ALU.mult)
            dve.tensor_scalar(bounds[:, T_PASSES:T_PASSES + 1], general, float(NT - 1), 1.0, ALU.mult, ALU.add)
            dve.tensor_scalar(bounds[:, T_ROUNDS:T_ROUNDS + 1], misc[:, 3:4], -1.0, float(ROUNDS), ALU.mult, ALU.add)
            dve.tensor_copy(bounds[:, T_START:T_START + 1], misc[:, 3:4])
            dve.tensor_copy(bounds[:, T_DENSE:T_DENSE + 1], misc[:, 0:1])
            dve.tensor_copy(bounds[:, T_GENERAL:T_GENERAL + 1], general).then_inc(s_bounds, 1)
            dve.wait_ge(s_stats, NT)
            me, mo, ve, vo = (stats[:, :, n] for n in (1, 4, 2, 5))
            a = st.mark(dve.tensor_tensor(sums, me, mo, ALU.add))
            b = st.mark(dve.tensor_tensor(diff, me, mo, ALU.subtract))
            c = st.mark(dve.tensor_tensor(var2, ve, vo, ALU.add))
            st.after(a)
            a = st.mark(dve.tensor_scalar(mean, sums, 0.5, None, ALU.mult))
            st.after(c)
            b = st.mark(dve.tensor_tensor(var, diff, diff, ALU.mult))
            st.after(b)
            b = st.mark(dve.scalar_tensor_tensor(out=std1b, in0=var, scalar=C / 4.0, in1=var2, op0=ALU.mult, op1=ALU.add))
            st.after(b)
            dve.tensor_scalar(var, std1b, 1.0 / C, None, ALU.mult).then_inc(s_var, 1)
            dve.wait_ge(s_std, 1)
            a = st.mark(dve.reciprocal(rstd[:, 0:NT], std1))
            st.after(a)
            a = st.mark(dve.tensor_tensor(sums, var, rstd[:, 0:NT], ALU.mult))
            st.after(a)
            dve.tensor_tensor(var2, sums, rstd[:, 0:NT], ALU.mult).then_inc(s_var, 1)
            dve.scalar_tensor_tensor(out=shift[:, 0:NT], in0=mean, scalar=-1.0, in1=rstd[:, 0:NT],
                                     op0=ALU.mult, op1=ALU.mult).then_inc(s_norm, 1)
            dve.wait_ge(s_std, 2)
            dve.reciprocal(gate_scale[:, 0:NT], stdg).then_inc(s_gs, 1)
            dve.wait_ge(s_small, SMALL)
            for k in range(KC):
                dve.tensor_scalar(wg1g[:, k, :], wg1[:, k, :], ln_g[:, k:k + 1], None, ALU.mult)
                last = dve.tensor_scalar(ln_bT[:, k, :], ones[:, 0:T], ln_b[:, k:k + 1], None, ALU.mult)
            last.then_inc(s_wprep, 1)

            with dve.Fori(0, NT // BODY) as i:
                st = Steps(dve, s_vec[1], i * STEPS_A, s_alone)
                for pr in range(BODY // 2):
                    t = i * BODY + 2 * pr
                    hold(dve, s_h, t + 2)
                    done, found = [None, None], [None, None]
                    for k in range(TOPK // 8):
                        for u in range(2):
                            src = h_psum(2 * pr + u) if k == 0 else taken[:, u, :]
                            if k:
                                st.after(done[u])
                            found[u] = st.mark(dve.max(top8[:, u * (TOPK // 8) + k, :], src))
                        for u in range(2):
                            src = h_psum(2 * pr + u) if k == 0 else taken[:, u, :]
                            st.after(found[u])
                            done[u] = st.mark(dve.match_replace(out=taken[:, u, :], in_to_replace=top8[:, u * (TOPK // 8) + k, :],
                                                                in_values=src, imm_value=BELOW))
                    dve.wait_ge(s_split, t + 2)
                    for u in range(2):
                        st.after(done[u])
                        last = dve.scalar_tensor_tensor(out=sparse[:, u, :], in0=taken[:, u, :], scalar=BELOW,
                                                        in1=h_psum(2 * pr + u), op0=ALU.is_equal, op1=ALU.mult)
                        last.then_inc(s_sparse, 1)
                dve.wait_ge(s_kvc, (i + 1) * BODY + 2)
                dve.tensor_reduce(kparts[:, bass.ds(i, 1), :].rearrange("p a c -> p (a c)"),
                                  k_all[:, bass.ds(i * BODY, BODY), :].rearrange("p t c -> p c t"), AX_X, ALU.max)\
                   .then_inc(s_kpart, 1)
            assert st.n == STEPS_A, st.n
            st = Steps(dve, s_vec[2])
            dve.wait_ge(s_kpart, NT // BODY)
            dve.tensor_reduce(kmax, kparts.rearrange("p a c -> p c a"), AX_X, ALU.max).then_inc(s_km, 1)
            dve.memset(v_all[:, 0:NT, :, 128:VH], 1.0).then_inc(s_vones, 1)
            dve.wait_ge(s_kmT, 1)
            a = st.mark(dve.tensor_reduce(kmaxT[:], bank[0][:, 0:KC * T].rearrange("p (k t) -> p k t", k=KC), AX_X, ALU.max))
            st.after(a)
            for k in range(KC):
                last = dve.tensor_scalar(kdiag[:, k, :], ident[:], kmaxT[:, k:k + 1], None, ALU.mult)
            last.then_inc(s_dg, 1)
            dve.wait_ge(s_kmb, 1)
            a = st.mark(dve.tensor_copy(kmaxb, bank[1][0:T, 0:C]))
            st.after(a)
            with dve.Fori(0, NT // 5) as i:
                ks = k_all[:, bass.ds(i * 5, 5), :]
                dve.tensor_tensor(ks, ks, kmaxb.rearrange("p (a c) -> p a c", a=1).to_broadcast([T, 5, C]), ALU.subtract)\
                   .then_inc(s_ksub, 1)
            dve.wait_ge(s_bounds, 1)
            dve.wait_ge(s_split, NT + 2)
            for p in range(2):
                dve.wait_ge(s_rows[p], 16 * (NT // 2 + 1))
            a = st.mark(dve.tensor_copy(src_lo_r, srcT[:, 0:CH]))
            st.after(a)
            a = st.mark(dve.tensor_scalar(keys_r, src_lo_r, -float(T // 2), 1.0 / T, ALU.add, ALU.mult))
            st.after(a)
            a = st.mark(dve.tensor_scalar(keys_r, keys_r, 1.5 * 2 ** 23, None, ALU.add))
            st.after(a)
            a = st.mark(dve.tensor_scalar(keys_r, keys_r, -1.5 * 2 ** 23, None, ALU.add))
            st.after(a)
            a = st.mark(dve.scalar_tensor_tensor(out=src_lo_r, in0=keys_r, scalar=-float(T), in1=src_lo_r, op0=ALU.mult, op1=ALU.add))
            st.after(a)
            a = st.mark(dve.scalar_tensor_tensor(out=keys_r, in0=dstT[:, GC:GC + CH], scalar=float(NT), in1=keys_r,
                                                 op0=ALU.mult, op1=ALU.add))
            st.after(a)
            dve.wait_ge(s_bg1, 1)
            dve.tensor_copy(bg1[:], bank[4][0:T, 0:GH]).then_inc(s_bg1c, 1)
            dve.wait_ge(s_ctx, 1)
            for h in range(KC):
                a = st.mark(dve.reciprocal(ctx_r[:, h:h + 1], bank[2 + h][:, 128:129]))
            st.after(a)
            for h in range(KC):
                for b in range(128 // HD):
                    d = slice(b * HD, (b + 1) * HD)
                    last = dve.tensor_scalar(ctx_bd[d, h, d], bank[2 + h][d, d], ctx_r[d, h:h + 1], None, ALU.mult)
            last.then_inc(s_bd, 1)
            dve.memset(x3, 0.0).then_inc(s_x3, 1)
            dve.memset(hgT[GH:GH + 1, :], 1.0)
            dve.memset(ones_row, 1.0)
            a = st.mark(dve.tensor_copy(src_lo, src_lo_r))
            b = st.mark(dve.tensor_copy(keys, keys_r))
            st.after(b)
            dve.wait_ge(s_wF, 16 * 5)
            dve.wait_ge(s_bg1c, 1)
            dve.wait_ge(s_gs, 1)
            dve.tensor_scalar(wproj, wproj, 0.5, None, ALU.mult).then_inc(s_ready, 1)

            def gate_pre(j, tile):
                dve.wait_ge(s_og, j + 1)
                dve.scalar_tensor_tensor(out=hg_pre, in0=bank[2][0:T, C:C + GH], scalar=gate_scale[:, bass.ds(tile, 1)],
                                         in1=bg1[:], op0=ALU.mult, op1=ALU.add).then_inc(s_hgpre, 1)

            def mix(j):
                dve.wait_ge(s_gate, j + 1)
                dve.scalar_tensor_tensor(out=mixed, in0=gate, scalar=1.0, in1=bank[2][0:T, 0:C],
                                         op0=ALU.add, op1=ALU.mult).then_inc(s_mix, 1)

            def ffn_rows(st, n, out):
                dve.wait_ge(s_y, n + 1)
                a = st.mark(dve.tensor_tensor(ybias, bank[6][0:T, C:2 * C], b2, ALU.add))
                st.after(a)
                dve.tensor_scalar(out, ybias, w_at[:, bass.ds(n, 1)], None, ALU.mult).then_inc(s_yw, 1)

            def visit(t, g, tile):
                at = dve.snap(((g + first_group) % NG) * GC + GC)
                visited = dve.snap((g + t) * GC)
                for s in range(GC):
                    dve.wait_ge(s_oh_free, visited + (s + 1))
                    dve.tensor_scalar(onehot[:, s, :], iota[:, 0:T], tile_start[:, bass.ds(tile, 1)],
                                      dstT[:, bass.ds(at + s, 1)], ALU.add, ALU.is_equal).then_inc(s_oh, 1)

            def window(i, k, part):
                w = i * NW + k
                pairs0 = load(dve, w + T_WIN, 0, NPAIR)
                pairs1 = load(dve, w + (T_WIN + 1), 0, NPAIR)
                middle = None if part is None else dve.snap((pairs0 + pairs1) // 2)

                def keys_of(c):
                    at = nc.s_assert_within(dve.snap(c * PAIR), 0, CH - PAIR,
                                            skip_runtime_bounds_check_because="the last pair is all padding")
                    visited = dve.snap((c + w) * PAIR)
                    for u in range(PAIR):
                        dve.wait_ge(s_hot_free, visited + (u + 1))
                        dve.tensor_scalar(lo_hot[:, u, :], iota[:, 0:T], src_lo[:, bass.ds(at + u, 1)], None, ALU.is_equal)
                        dve.tensor_scalar(key_hot[:, u, :], iota[:, 0:KEYS], win_flat[:, bass.ds(w, 1)],
                                          keys[:, bass.ds(at + u, 1)], ALU.add, ALU.is_equal).then_inc(s_hot, 1)

                if part == 0:
                    with dve.If(middle > pairs0):
                        with dve.Fori(pairs0, middle) as c:
                            keys_of(c)
                    return
                with dve.Fori(middle if part == 1 else pairs0, pairs1 + 1) as c:
                    keys_of(c)

            win_flat = win_start[:].rearrange("p a b -> p (a b)")
            gate_pre(0, tile_at(0, 0))
            mix(0)
            ends = Ends(dve)
            first_group = load(dve, T_FIRST, 0, NG)
            general = load(dve, T_GENERAL, 0, 1)
            def position(n, tile, after, u, half, i, windows, from_counts, s, last):
                g0, g1, finals = ends.enter(n, s)

                def gathered():
                    cuts, parts = [g0], [part for k in windows for part in ([(k, 0), (k, 1)] if k == 0 else [(k, None)])]
                    if parts:
                        cuts.append(dve.snap((g0 + g1) // 2))
                    if len(parts) > 1:
                        cuts.insert(1, dve.snap((g0 + cuts[1]) // 2))
                    cuts.append(g1)
                    for at, (first, end) in enumerate(zip(cuts, cuts[1:])):
                        with dve.If(end > first):
                            with dve.Fori(first, end) as g:
                                visit(finals, g, tile)
                        if at < len(parts):
                            window(i, *parts[at])
                    visit(finals, g1, tile)

                if not from_counts:
                    gathered()
                else:
                    with dve.If(general > 0):
                        gathered()
                st = Steps(dve, s_vec[3], n * STEPS_C)
                dve.wait_ge(s_xin, (n + 1) * 16)
                a = st.mark(dve.tensor_tensor(base_x, xin, bproj, ALU.add))
                dve.wait_ge(s_p, n + 1)
                st.after(a)
                a = st.mark(dve.tensor_tensor(base_p, base_x, bank[6][0:T, 0:C], ALU.add))
                hold(dve, s_ywout[u], (half + 1) * 16)
                ffn_rows(st, n, yw[:, u, :])
                dve.wait_ge(s_agg, n + 1)
                dve.tensor_scalar(col["deg"][:], bank[1][0:T, 0:1], 1.0, None, ALU.max).then_inc(s_deg, 1)
                c = st.mark(dve.tensor_copy(junk, bank[0][0:T, 0:C]))
                dve.wait_ge(s_deg, n + 1)
                b = st.mark(dve.reciprocal(col["rdeg"][:], col["deg"][:]))
                st.after(c)
                c = st.mark(dve.scalar_tensor_tensor(out=agg_sum, in0=bank[0][0:T, C:2 * C], scalar=1.0 / LO_SCALE,
                                                     in1=junk, op0=ALU.mult, op1=ALU.add))
                st.after(c)
                a = st.mark(dve.scalar_tensor_tensor(out=x2, in0=agg_sum, scalar=col["rdeg"][:, 0:1], in1=base_p,
                                                     op0=ALU.mult, op1=ALU.add))
                st.after(a)
                gate_pre(n + 1, after)
                a = st.mark(dve.bn_stats(bn6[:], x2))
                hold(dve, s_vec[3], n * STEPS_C + a)
                a = st.mark(dve.bn_aggr(mv[:], bn6[:]))
                st.after(a)
                dve.sem_inc(s_v2, 1)
                a = st.mark(dve.tensor_scalar(scaled[0], mv[:, 1:2], EPS, None, ALU.add))
                st.after(a)
                st.mark(dve.tensor_scalar(scaled[1], scaled[0], 1.0 / 4, None, ALU.mult))
                st.mark(dve.tensor_scalar(scaled[2], scaled[0], 1.0 / 16, None, ALU.mult))
                a = st.mark(dve.tensor_scalar(halved, scaled[0].bitcast(I32), 1, None, ALU.logical_shift_right))
                st.after(a)
                a = st.mark(dve.tensor_scalar(root.bitcast(I32), halved, -1.0, float(0x5f3759df), ALU.mult, ALU.add))
                st.after(a)
                for k in range(3):
                    a = st.mark(dve.tensor_scalar(square, root, root, scaled[k], ALU.mult, ALU.mult))
                    st.after(a)
                    a = st.mark(dve.scalar_tensor_tensor(out=root, in0=square, scalar=3.0, in1=root, op0=ALU.subtract, op1=ALU.mult))
                    st.after(a)
                a = st.mark(dve.tensor_scalar(col["rstd"][:], root, -1.0 / 8, None, ALU.mult))
                st.after(a)
                hold(dve, s_tx3, n + 1)
                a = st.mark(dve.tensor_scalar(x3, x2, mv[:, 0:1], col["rstd"][:, 0:1], ALU.subtract, ALU.mult))
                st.after(a)
                dve.sem_inc(s_x3, 1)
                a = st.mark(dve.tensor_tensor_reduce(out=junk, in0=x3, in1=wr, scale=1.0, scalar=0.0, op0=ALU.mult,
                                                     op1=ALU.add, accum_out=col["w"][:]))
                dve.tensor_tensor(res_all[:, bass.ds(tile, 1), :], x2.rearrange("p (a c) -> p a c", a=1),
                                  x3.rearrange("p (a c) -> p a c", a=1), ALU.add).then_inc(s_res, 1)
                st.after(a)
                b = st.mark(dve.tensor_scalar(w_all[:, bass.ds(tile, 1)], col["w"][:], br[:, 0:1], None, ALU.add))
                a = st.mark(dve.tensor_scalar(w_at[:, bass.ds(n + 2, 1)], col["w"][:], br[:, 0:1], None, ALU.add))
                st.after(a)
                mix(n + 1)
                ends.look_ahead(n, last)
                assert st.n == STEPS_C, st.n

            positions(dve, position)
            st = Steps(dve, s_vec[4])
            w = w_all[:]
            c = {n: col[n][:, 0:1] for n in col}
            dve.tensor_scalar(hit, w, 0.0, 0.0, ALU.is_ge, ALU.add, accum_out=c["cnt"]).then_inc(s_cnt, 1)
            dve.wait_ge(s_p, NT + 1)
            ffn_rows(st, NT, yw_all[:, NT - 2, :])
            dve.wait_ge(s_tot, 1)
            a = st.mark(dve.tensor_scalar(c["pos"], bank[0][0:T, 0:1], float(KEEP), None, ALU.is_ge))
            st.after(a)
            a = st.mark(dve.tensor_scalar(c["sgn"], c["pos"], 2.0, -1.0, ALU.mult, ALU.add))
            b = st.mark(dve.tensor_scalar(c["goal"], c["pos"], float(2 * KEEP - N - 1), float(N - KEEP + 1), ALU.mult, ALU.add))
            st.after(a)
            a = st.mark(dve.tensor_scalar(wv, w, c["sgn"], None, ALU.mult))
            top = 31 - DIGIT
            dve.memset(best[:], 0)
            for n in range(CANDS):
                dve.memset(cand[:, n:n + 1], (n + 1) << top)
                b = st.mark(dve.memset(digits[:, n:n + 1], (n + 1) << top))
            b = st.mark(dve.memset(c["bit"], float(1 << top)))
            st.after(b)

            def count(n):
                return dve.tensor_scalar(hit_n[:, n, :], wv, cand[:, n:n + 1].bitcast(F32), 0.0, ALU.is_ge, ALU.add,
                                         accum_out=counts[:, n:n + 1])

            base0 = st.n
            with dve.Fori(0, ROUNDS_D) as i:
                st = Steps(dve, s_vec[4], i * STEPS_D + base0)
                for n in range(CANDS):
                    last = count(n)
                last.then_inc(s_cnt, 1)
                a = st.mark(dve.tensor_scalar(digits[:, 0:CANDS], digits[:, 0:CANDS], DIGIT, None, ALU.logical_shift_right))
                dve.wait_ge(s_tot, i + 2)
                b = st.mark(dve.tensor_scalar(over[:, 0:CANDS], bank[0][0:T, 0:CANDS], c["goal"], 0.0, ALU.is_ge, ALU.add,
                                              accum_out=c["pos"]))
                st.after(b)
                b = st.mark(dve.tensor_scalar(accept[:], c["pos"], c["bit"], None, ALU.mult))
                st.after(b)
                b = st.mark(dve.tensor_tensor(best[:], best[:], accept[:], ALU.bitwise_or))
                a = st.mark(dve.tensor_scalar(c["bit"], c["bit"], 1.0 / 2 ** DIGIT, None, ALU.mult))
                st.after(b)
                b = st.mark(dve.tensor_tensor(cand[:, 0:CANDS], best[:].to_broadcast([T, CANDS]), digits[:, 0:CANDS], ALU.bitwise_or))
                st.after(b)
            assert st.n == STEPS_D, st.n
            st = Steps(dve, s_vec[4], base0 + ROUNDS_D * STEPS_D)
            a = st.mark(dve.memset(accept[:], 1))
            st.after(a)
            a = st.mark(dve.tensor_tensor(cand[:, 0:1], best[:], accept[:], ALU.bitwise_or))
            st.after(a)
            count(0).then_inc(s_cnt, 1)
            dve.wait_ge(s_tot, ROUNDS_D + 2)
            a = st.mark(dve.tensor_scalar(accept[:], bank[0][0:T, 0:1], c["goal"], None, ALU.is_ge))
            st.after(a)
            a = st.mark(dve.tensor_tensor(best[:], best[:], accept[:], ALU.bitwise_or))
            st.after(a)
            a = st.mark(dve.tensor_scalar(c["thr"], best[:].bitcast(F32), c["sgn"], None, ALU.mult))
            st.after(a)
            a = st.mark(dve.tensor_scalar(gtm, w, c["thr"], 0.0, ALU.is_gt, ALU.add, accum_out=c["cnt"]))
            b = st.mark(dve.tensor_scalar(eqm, w, c["thr"], None, ALU.is_equal))
            st.after(b)
            dve.sem_inc(s_cnt, 1)
            dve.wait_ge(s_tot, ROUNDS_D + 3)
            a = st.mark(dve.tensor_scalar(c["need"], bank[0][0:T, 0:1], -1.0, float(KEEP), ALU.mult, ALU.add))
            b = st.mark(dve.tensor_tensor_scan(colcum, ones_row, bank[1][0:T, 0:NT], 0.0, ALU.mult, ALU.add))
            st.after(b)
            b = st.mark(dve.tensor_tensor(colcum, colcum, bank[1][0:T, 0:NT], ALU.subtract))
            st.after(b)
            b = st.mark(dve.tensor_tensor(prefix, colcum, bank[2][0:T, 0:NT], ALU.add))
            st.after(b)
            b = st.mark(dve.scalar_tensor_tensor(out=hit, in0=prefix, scalar=c["need"], in1=eqm, op0=ALU.is_lt, op1=ALU.mult))
            st.after(b)
            b = st.mark(dve.tensor_tensor(selm, hit, gtm, ALU.add))
            st.after(b)
            ffn_rows(st, NT + 1, yw_all[:, NT - 1, :])
            dve.wait_ge(s_yw, NT + 3)
            dve.wait_ge(s_res, NT)
            dve.wait_ge(s_ywin, 16 * (2 * ND + 1))
            for t in range(NT):
                dve.scalar_tensor_tensor(out=res_all[:, t, :], in0=yw_all[:, t, :], scalar=selm[:, t:t + 1],
                                         in1=res_all[:, t, :], op0=ALU.mult, op1=ALU.add).then_inc(s_fin, 1)


_INS = ["x", "src", "dst", "L0_gnn_W_self", "L0_gnn_W_neigh", "L0_mix_Wqkv", "L0_mix_Wproj", "L0_mix_bproj",
        "L0_mix_ln_g", "L0_mix_ln_b", "L0_mix_Wg1", "L0_mix_bg1", "L0_mix_Wg2", "L0_mix_bg2",
        "L0_ffn_attention_mask", "L0_ffn_wr", "L0_ffn_br", "L0_ffn_w1", "L0_ffn_b1", "L0_ffn_w2", "L0_ffn_b2"]


def kernel(**inputs):
    import numpy as _np
    import concourse.bacc as _bacc
    from concourse import mybir as _mybir
    from concourse.bass_utils import run_bass_kernel_spmd as _run

    nc = _bacc.Bacc("TRN2", target_bir_lowering=False, num_devices=1)
    arrays, args = {}, []
    for name in _INS:
        a = _np.ascontiguousarray(inputs[name])
        arrays[f"in_{name}_dram"] = a
        args.append(nc.dram_tensor(f"in_{name}_dram", a.shape, _mybir.dt.from_np(a.dtype), kind="ExternalInput").ap())
    out = nc.dram_tensor("out_dram", inputs["x"].shape, _mybir.dt.float32, kind="ExternalOutput").ap()
    build(nc, *args, out)
    r = _run(nc, [arrays], core_ids=[0])
    return r.results[0]["out_dram"]
```
